# Optimizing a Trainium2 kernel written in Bass

```python
import numpy as np
import jax
import jax.numpy as jnp

def _softmax(x, axis=-1):
    return jax.nn.softmax(x, axis=axis)

def _gelu(x):
    return jax.nn.gelu(x, approximate=True)

def _silu(x):
    return jax.nn.silu(x)

def _sigmoid(x):
    return jax.nn.sigmoid(x)

def _layernorm(x, axis=-1, eps=1e-05):
    m = jnp.mean(x, axis=axis, keepdims=True)
    v = jnp.var(x, axis=axis, keepdims=True)
    return (x - m) / jnp.sqrt(v + eps)

def _scatter_add(tgt, idx, src, axis=0):
    return tgt.at[idx].add(src)

def _segment_sum(src, seg, n):
    return jax.ops.segment_sum(src, seg, n)
kernel_name = 'mk_prb_d1_jaxref_r8_52eec8'

def setup_inputs(seed: int=0):
    np.random.seed(seed)
    _w = jnp.asarray

    def _L0_attn_setup():
        import jax, jax.numpy as jnp
        import numpy as np
        D = 128
        H = 16
        DK = D // H
        CHUNK = 64
        EPS = 1e-05

        def _layernorm_noaffine(k):
            mu = jnp.mean(k, axis=-1, keepdims=True)
            var = jnp.mean((k - mu) ** 2, axis=-1, keepdims=True)
            return (k - mu) / jnp.sqrt(var + EPS)

        def _linear_attn(x, W_qkv, W_o):
            B, L, Dm = x.shape
            qkv = (x @ W_qkv).reshape(B, L, 3, H, DK)
            q, k, v = (qkv[:, :, 0], qkv[:, :, 1], qkv[:, :, 2])
            k = _layernorm_noaffine(k)
            nC = L // CHUNK
            to_chunks = lambda t: t.reshape(B, nC, CHUNK, H, DK).transpose(1, 0, 2, 3, 4)
            qc, kc, vc = (to_chunks(q), to_chunks(k), to_chunks(v))
            causal = jnp.tril(jnp.ones((CHUNK, CHUNK), dtype=bool))

            def step(S, chunk):
                q_c, k_c, v_c = chunk
                inter = jnp.einsum('bhde,bthe->bthd', S, q_c)
                scores = jnp.einsum('bthd,bshd->bhts', q_c, k_c)
                scores = jnp.where(causal, scores, 0.0)
                intra = jnp.einsum('bhts,bshd->bthd', scores, v_c)
                S = S + jnp.einsum('bthd,bthe->bhde', v_c, k_c)
                return (S, inter + intra)
            S0 = jnp.zeros((B, H, DK, DK), dtype=x.dtype)
            _, ys = jax.lax.scan(step, S0, (qc, kc, vc))
            y = ys.transpose(1, 0, 2, 3, 4).reshape(B, L, Dm)
            return y @ W_o
        key = jax.random.key(seed)
        k1, k2, k3 = jax.random.split(key, 3)
        x = jax.random.normal(k1, (4, 512, D), dtype=jnp.float32)
        W_qkv = jax.random.normal(k2, (D, 3 * D), dtype=jnp.float32) * 0.02
        W_o = jax.random.normal(k3, (D, D), dtype=jnp.float32) * 0.02
        return {'x': x, 'W_qkv': W_qkv, 'W_o': W_o}
    _L0_attn_in = _L0_attn_setup()

    def _L0_ffn_setup():
        import jax, jax.numpy as jnp
        import numpy as np
        E, D, F = (8, 128, 512)
        LN_EPS = 1e-05
        key = jax.random.key(seed)
        k = jax.random.split(key, 8)
        x = jax.random.normal(k[0], (4, 256, D), jnp.float32)
        centroids = jax.random.normal(k[1], (E, D), jnp.float32) * 0.1
        ln_g = jnp.ones((E, D), jnp.float32)
        ln_b = jnp.zeros((E, D), jnp.float32)
        w1 = jax.random.normal(k[2], (E, F, D), jnp.float32) * (1.0 / np.sqrt(D))
        b1 = jnp.zeros((E, F), jnp.float32)
        w2 = jax.random.normal(k[3], (E, D, F), jnp.float32) * (1.0 / np.sqrt(F))
        b2 = jnp.zeros((E, D), jnp.float32)
        return {'input_features': x, 'centroids': centroids, 'ln_g': ln_g, 'ln_b': ln_b, 'w1': w1, 'b1': b1, 'w2': w2, 'b2': b2}
    _L0_ffn_in = _L0_ffn_setup()
    _d = {'L0_attn_x': _L0_attn_in['x'], 'L0_attn_W_qkv': _L0_attn_in['W_qkv'], 'L0_attn_W_o': _L0_attn_in['W_o'], 'L0_ffn_centroids': _L0_ffn_in['centroids'], 'L0_ffn_ln_g': _L0_ffn_in['ln_g'], 'L0_ffn_ln_b': _L0_ffn_in['ln_b'], 'L0_ffn_w1': _L0_ffn_in['w1'], 'L0_ffn_b1': _L0_ffn_in['b1'], 'L0_ffn_w2': _L0_ffn_in['w2'], 'L0_ffn_b2': _L0_ffn_in['b2']}
    _x0 = _d['L0_attn_x']
    _d['L0_attn_x'] = jax.random.normal(jax.random.fold_in(jax.random.key(seed), 1), (8, 1024, 128), dtype=_x0.dtype)
    del _x0
    return _d

def reference(L0_attn_x, L0_attn_W_qkv, L0_attn_W_o, L0_ffn_centroids, L0_ffn_ln_g, L0_ffn_ln_b, L0_ffn_w1, L0_ffn_b1, L0_ffn_w2, L0_ffn_b2):

    def _L0_attn_ref(x, W_qkv, W_o):
        import jax, jax.numpy as jnp
        import numpy as np
        D = 128
        H = 16
        DK = D // H
        CHUNK = 64
        EPS = 1e-05

        def _layernorm_noaffine(k):
            mu = jnp.mean(k, axis=-1, keepdims=True)
            var = jnp.mean((k - mu) ** 2, axis=-1, keepdims=True)
            return (k - mu) / jnp.sqrt(var + EPS)

        def _linear_attn(x, W_qkv, W_o):
            B, L, Dm = x.shape
            qkv = (x @ W_qkv).reshape(B, L, 3, H, DK)
            q, k, v = (qkv[:, :, 0], qkv[:, :, 1], qkv[:, :, 2])
            k = _layernorm_noaffine(k)
            nC = L // CHUNK
            to_chunks = lambda t: t.reshape(B, nC, CHUNK, H, DK).transpose(1, 0, 2, 3, 4)
            qc, kc, vc = (to_chunks(q), to_chunks(k), to_chunks(v))
            causal = jnp.tril(jnp.ones((CHUNK, CHUNK), dtype=bool))

            def step(S, chunk):
                q_c, k_c, v_c = chunk
                inter = jnp.einsum('bhde,bthe->bthd', S, q_c)
                scores = jnp.einsum('bthd,bshd->bhts', q_c, k_c)
                scores = jnp.where(causal, scores, 0.0)
                intra = jnp.einsum('bhts,bshd->bthd', scores, v_c)
                S = S + jnp.einsum('bthd,bthe->bhde', v_c, k_c)
                return (S, inter + intra)
            S0 = jnp.zeros((B, H, DK, DK), dtype=x.dtype)
            _, ys = jax.lax.scan(step, S0, (qc, kc, vc))
            y = ys.transpose(1, 0, 2, 3, 4).reshape(B, L, Dm)
            return y @ W_o
        return _linear_attn(x, W_qkv, W_o)

    def _L0_ffn_ref(input_features, centroids, ln_g, ln_b, w1, b1, w2, b2):
        import jax, jax.numpy as jnp
        import numpy as np
        E, D, F = (8, 128, 512)
        LN_EPS = 1e-05
        x = input_features.reshape(-1, D)
        aff = jax.lax.stop_gradient(x) @ centroids.T
        assign = jnp.argmax(aff, axis=1)
        onehot = jax.nn.one_hot(assign, E, dtype=x.dtype)
        mu = jnp.mean(x, axis=-1, keepdims=True)
        var = jnp.mean((x - mu) ** 2, axis=-1, keepdims=True)
        xhat = (x - mu) * jax.lax.rsqrt(var + LN_EPS)
        xn = xhat[None, :, :] * ln_g[:, None, :] + ln_b[:, None, :]
        h = jax.nn.relu(jnp.einsum('etd,efd->etf', xn, w1) + b1[:, None, :])
        y = x[None, :, :] + jnp.einsum('etf,edf->etd', h, w2) + b2[:, None, :]
        alpha = jax.nn.sigmoid(x @ centroids.T)
        a = alpha.T[:, :, None]
        gated = a * y + (1.0 - a) * x[None, :, :]
        out = jnp.einsum('te,etd->td', onehot, gated)
        return out.reshape(input_features.shape)
    x = L0_attn_x
    xn = _layernorm(x, axis=-1)
    x = x + _L0_attn_ref(xn, L0_attn_W_qkv, L0_attn_W_o) + _L0_ffn_ref(xn, L0_ffn_centroids, L0_ffn_ln_g, L0_ffn_ln_b, L0_ffn_w1, L0_ffn_b1, L0_ffn_w2, L0_ffn_b2)
    return x

_drawn_inputs = setup_inputs


def setup_inputs(seed=0):
    import zlib

    import numpy as np

    out = dict(_drawn_inputs(seed))
    spreads = {'L0_ffn_ln_g': (1.0, 0.2),
     'L0_ffn_ln_b': (0.0, 0.364),
     'L0_ffn_b1': (0.0, 0.375),
     'L0_ffn_b2': (0.0, 0.271)}
    factors = {}
    for name, (base, spread) in spreads.items():
        noise = np.random.default_rng([zlib.crc32(name.encode()), seed]).standard_normal(out[name].shape)
        drawn = base * np.exp(spread * noise) if base else spread * noise
        out[name] = jnp.asarray(drawn.astype(out[name].dtype))
    for name, factor in factors.items():
        out[name] = (out[name] * factor).astype(out[name].dtype)
    return out
```

```python
import concourse.bass as bass
from concourse import mybir
from contextlib import ExitStack

F32, F16, BF16, I32, U32 = (mybir.dt.float32, mybir.dt.float16, mybir.dt.bfloat16, mybir.dt.int32, mybir.dt.uint32)
ALU = mybir.AluOpType
ACT = mybir.ActivationFunctionType
AX = mybir.AxisListType.X


def reach(eng, sem, value):
    if isinstance(value, int) and value <= 0:
        return
    eng.wait_ge(sem, value)


def reach_alone(eng, sem, value, passed):
    if isinstance(value, int) and value <= 0:
        return
    eng.wait_ge(sem, value)
    if not isinstance(value, int):
        eng.sem_inc(passed, 1)


def moe_attention_kernel(nc, x, w_qkv, w_o, centroids, ln_g, ln_b, w1, b1, w2, b2, out):
    B, L, D = x.shape
    E, F, _ = w1.shape
    P = 128
    H = 16
    DK = D // H
    NCH = L // P
    NT = B * NCH
    NTOK = B * L
    HALF = B // 2
    NQ = NT // HALF
    G = P // 32
    J = H // G
    FC = F // P
    NS = NT + E
    ROW = D + 4
    EPS = 1e-5
    QTOP = 1024.0
    TINY = 1e-30

    x_v = x.rearrange("b (c p) d -> p c b d", p=P)
    slots_d = nc.dram_tensor("slots_d", (NS * P, ROW), F32, kind="Internal").ap()
    attn_d = nc.dram_tensor("attn_d", (NTOK, D), F32, kind="Internal").ap()
    attn_v = attn_d.rearrange("(b c p) d -> p c b d", p=P, c=NCH)
    slots_v = slots_d.rearrange("(k p) r -> p k r", p=P)
    out_rows = out.rearrange("b l d -> (b l) d")

    ctx = ExitStack()
    with ctx:
        def sb(name, shape, dt=F32):
            return ctx.enter_context(nc.sbuf_tensor(name, shape, dt))

        def sem(name):
            return ctx.enter_context(nc.semaphore(name))

        resid = sb("resid", [P, NT, D])
        rows = sb("rows", [P, NT, ROW])
        w1t = sb("w1t", [P, E, F])
        b1b = sb("b1b", [P, E, F])
        w2t = sb("w2t", [P, E, FC, D])
        b2b = sb("b2b", [P, E, D])
        pos_i = sb("pos_i", [P, NT], I32)
        eid_i = sb("eid_i", [P, NS], I32)
        wqkv = sb("wqkv", [P, 3 * D])
        wo = sb("wo", [P, D])
        wom = sb("wom", [P, J, D])
        ident = sb("ident", [P, P])
        identh = sb("identh", [P, P], F16)
        causal = sb("causal", [P, P])
        headmask = sb("headmask", [P, P])
        jmask = sb("jmask", [P, J])
        eps = sb("eps", [P, 1])
        ones = sb("ones", [P, P])
        zrow = sb("zrow", [P, ROW])

        stats = sb("stats", [P, 2, B, 6])
        mv = sb("mv", [P, 2, B, 2])
        std = sb("std", [P, 2, B])
        rs_s = sb("rs_s", [P, 2, B])
        cen_t = sb("cen_t", [P, E])
        g_t = sb("g_t", [P, E])
        lb_t = sb("lb_t", [P, E])
        var_all = sb("var_all", [P, NT])
        rstd_all = sb("rstd_all", [P, NT])
        tmp_nt = sb("tmp_nt", [P, NT])
        tmp_nt2 = sb("tmp_nt2", [P, NT])
        pr = sb("pr", [P, G, J * P])
        pr_v = pr[:, :, :].rearrange("p g (j t) -> p g j t", j=J)
        xq = sb("xq", [P, 2, HALF, ROW])
        xt = sb("xt", [P, HALF, P])
        q32 = sb("q32", [P, HALF * D])
        kv32 = sb("kv32", [P, 4, HALF * D])
        k32, v32 = kv32[:, 0:2, :], kv32[:, 2:4, :]
        sq = sb("sq", [P, HALF * D])
        kvar = sb("kvar", [P, HALF * H])
        kstd = sb("kstd", [P, HALF * H])
        krs = sb("krs", [P, HALF * H])
        qs = sb("qs", [P, 2, HALF * H, 4, DK], F16)
        ks = sb("ks", [P, 2, HALF * H, 4, DK], F16)
        qqt = sb("qqt", [P, 2, J, P], F16)
        kkt = sb("kkt", [P, 2, J, P], F16)
        qt = sb("qt", [P, HALF, P])
        yint = sb("yint", [P, HALF, P])
        ys = sb("ys", [P, 2, J, P])
        state = sb("state", [P, B, P])
        dstate = sb("dstate", [P, HALF, P])
        res = sb("res", [P, 2, HALF, D])
        idxq = sb("idxq", [P, 2, HALF], I32)

        lnx = kv32[:, :, :].rearrange("p a n -> p (a n)").rearrange("p (a b d) -> p a b d", a=2, b=B)
        xta = ys

        wraw = sq[:, 0:3 * D]

        aff = pr[:, 0, :].rearrange("p (t e) -> p t e", e=E)
        rt1 = pr[:, 1, :].rearrange("p (t e) -> p t e", e=E)
        rt2 = pr[:, 2, :].rearrange("p (t e) -> p t e", e=E)
        rt3 = pr[:, 3, :].rearrange("p (t e) -> p t e", e=E)
        rt4 = q32[:, :].rearrange("p (t e) -> p t e", e=E)
        eidf = kv32[:, 0:2, :].rearrange("p a n -> p (a n)")[:, 0:NS * E].rearrange("p (k e) -> p k e", e=E)
        ohb = sb("ohb", [P, NT, E], BF16)
        before = sb("before", [P, P], BF16)
        onesb = sb("onesb", [P, P], BF16)
        desc = sb("desc", [P, E])
        iot_i = sb("iot_i", [P, NS], I32)
        iotk = sb("iotk", [P, NS])
        cnt = sb("cnt", [P, 5, E])
        mx = sb("mx", [P, NT])
        id_i = sb("id_i", [P, NT], I32)

        w1raw = state[:, :, :].rearrange("p (a c) d -> p a c d", a=2)
        w2raw = res[:, :, :, :].rearrange("p a b d -> p a (b d)")
        b1row = [dstate[0:1, :, :].rearrange("p a b -> p (a b)"), yint[0:1, :, :].rearrange("p a b -> p (a b)")]
        w1tr = xt[:, :, :].rearrange("p a b -> p (a b)")
        lbb = qt[:, 0, :]

        xs = sb("xs", [P, 4, ROW])
        xse = sb("xse", [P, 2, P])
        hb, ht = pr[:, 0:2, :], pr[:, 2:4, :]
        idxe = sb("idxe", [P, 4], I32)
        att = sb("att", [P, 4, D])
        ye = sb("ye", [P, 4, D])
        yb = sb("yb", [P, 2, D])

        banks = [ctx.enter_context(nc.psum_tensor(f"bank{i}", [P, 512], F32)) for i in range(8)]

        S = {}

        def bcast(v, axis, n):
            shape = list(v.shape)
            return v.unsqueeze(axis).to_broadcast(shape[:axis] + [n] + shape[axis:])

        def s(name):
            if name not in S:
                S[name] = sem(name)
            return S[name]

        block = ctx.enter_context(nc.Block())

        SC = [banks[0], banks[1]]
        YB, QB, KB, CB, EB, DB = banks[2], banks[3], banks[4], banks[5], banks[6], banks[7]
        qb16 = QB[:, 0:256].bitcast(F16).rearrange("p (j t) -> p j t", j=J)
        kb16 = KB[:, 0:256].bitcast(F16).rearrange("p (j t) -> p j t", j=J)

        @block.sync
        def _(sp):
            sp.dma_start(wraw, w_qkv).then_inc(s("wqkv_in"), 16)
            sp.dma_start(wo[:, :], w_o).then_inc(s("wo_in"), 16)

            def load_x(c, a):
                reach(sp, s("stats_done"), c - 1)
                sp.dma_start(resid[:, bass.ds(c * B, B), :], x_v[:, c, :, :]).then_inc(s(f"x_in{a}"), 16)

            load_x(0, 0)
            load_x(1, 1)
            with sp.Fori(1, NCH // 2, 1) as i:
                for a in range(2):
                    load_x(2 * i + a, a)

            def load_expert(e, a):
                    reach(sp, s("b1_ps"), e - 1)
                    sp.dma_start(w1raw[:, a, :, :], w1.rearrange("e (c p) d -> p e c d", p=P)[:, e, :, :])\
                      .then_inc(s(f"wraw_in{a}"), 16)
                    sp.dma_start(w2raw[:, a, :], w2.rearrange("e d f -> d e f")[:, e, :]).then_inc(s(f"wraw_in{a}"), 16)
                    sp.dma_start(b1row[a], b1.rearrange("(o e) f -> o e f", o=1)[:, e, :])\
                      .then_inc(s(f"wraw_in{a}"), 16)

            load_expert(0, 0)
            load_expert(1, 1)
            with sp.Fori(1, E // 2, 1) as i:
                for a in range(2):
                    load_expert(2 * i + a, a)

            def store_quad(n, c, half):
                sp.wait_ge(s("res_ready"), n + 1)
                sp.dma_start(attn_v[:, c, half * HALF:(half + 1) * HALF, :], res[:, half, :, :])\
                  .then_inc(s(f"attn_out{half}"), 16)

            with sp.Fori(0, NCH, 1) as c:
                for half in range(2):
                    store_quad(2 * c + half, c, half)

            for half in range(2):
                sp.wait_ge(s(f"scattered{half}"), 16 * HALF * NCH)

            def load_slots(k, kk):
                reach(sp, s("ye_ready"), k - 3)
                sp.dma_start(xs[:, kk % 4, :], slots_v[:, k, :]).then_inc(s(f"se_in{kk % 4}"), 16)

            for k in range(4):
                load_slots(k, k)
            with sp.Fori(1, NS // 4, 1) as i:
                for a in range(4):
                    load_slots(4 * i + a, a)
            for a in range(4):
                sp.wait_ge(s(f"out_done{a}"), 16 * (NS // 4))

        @block.gpsimd
        def _(pool):
            pool.memset(ident[:, :], 0.0).then_inc(s("pool_c"), 1)
            pool.memset(causal[:, :], 1.0).then_inc(s("pool_c"), 1)
            pool.memset(headmask[:, :], 1.0).then_inc(s("pool_c"), 1)
            pool.memset(jmask[:, :], 1.0).then_inc(s("pool_c"), 1)
            pool.memset(rt1[:, :, :], 1.0).then_inc(s("pool_c"), 1)
            pool.memset(zrow[:, :], 0.0).then_inc(s("pool_c"), 1)
            pool.wait_ge(s("pool_c"), 6)
            pool.affine_select(out=ident[:, :], in_=ident[:, :], compare_op=ALU.not_equal, fill=1.0, base=0,
                               pattern=[[-1, P]], channel_multiplier=1).then_inc(s("ident_ready"), 1)
            pool.dma_start(slots_v, bcast(zrow[:, :], 1, NS))\
                .then_inc(s("slots_zero"), 16)
            pool.dma_start(b2b[:, :, :], b2.partition_broadcast(P)).then_inc(s("b2_in"), 16)
            pool.affine_select(out=causal[:, :], in_=causal[:, :], compare_op=ALU.is_ge, fill=0.0, base=0,
                               pattern=[[1, P]], channel_multiplier=-1).then_inc(s("pool_m"), 1)
            hm = headmask[:, :].rearrange("p (g j d) -> p g j d", g=G, d=DK)
            pool.affine_select(out=hm, in_=hm, compare_op=ALU.is_ge, fill=0.0, base=0,
                               pattern=[[-DK, G], [-32, J], [0, DK]], channel_multiplier=1).then_inc(s("pool_m"), 1)
            ones_v = rt1.rearrange("p t e -> p (t e)")
            pool.affine_select(out=ones_v[:, 0:P], in_=ones_v[:, 0:P], compare_op=ALU.is_ge, fill=0.0, base=-1,
                               pattern=[[1, P]], channel_multiplier=-1).then_inc(s("pool_m"), 1)
            jm = ones_v[:, P:P + H].rearrange("p (g j) -> p g j", g=G)
            pool.affine_select(out=jm, in_=jm, compare_op=ALU.is_ge, fill=0.0, base=0,
                               pattern=[[-32, G], [-DK, J]], channel_multiplier=1).then_inc(s("pool_m"), 1)
            pool.wait_ge(s("pool_m"), 4)
            pool.affine_select(out=hm, in_=hm, compare_op=ALU.is_ge, fill=0.0, base=DK - 1,
                               pattern=[[DK, G], [32, J], [0, DK]], channel_multiplier=-1).then_inc(s("pool_m"), 1)
            pool.affine_select(out=jm, in_=jm, compare_op=ALU.is_ge, fill=0.0, base=DK - 1,
                               pattern=[[32, G], [DK, J]], channel_multiplier=-1).then_inc(s("pool_m"), 1)
            pool.iota(iot_i[:, :], [[1, NS]], base=0, channel_multiplier=0).then_inc(s("pool_m"), 1)
            pool.iota(id_i[:, :].rearrange("p (c b) -> p c b", b=B), [[-P, NCH], [-L, B]], base=NTOK,
                      channel_multiplier=-1).then_inc(s("pool_m"), 1)

            def add_resid(i, a):
                pool.wait_ge(s("lnx_ready"), 2 * i + a + 1)
                t0 = (2 * i + a) * B
                pool.tensor_tensor(resid[:, bass.ds(t0, B), :], resid[:, bass.ds(t0, B), :], lnx[:, a, :, :], ALU.add)\
                    .then_inc(s("resid_ready"), 1)

            with pool.Fori(0, NCH // 2, 1) as i:
                for a in range(2):
                    add_resid(i, a)

            def split_high(src, dst, done):
                pool.tensor_scalar(dst, src, 1.0, 0.0, ALU.mult, ALU.add).then_inc(done, 1)

            def q_high(n, par):
                reach_alone(pool, s("q_sb"), n + 1, s("pool_passed"))
                reach_alone(pool, s("qk_ps"), 4 * (n - 1), s("pool_passed"))
                split_high(q32[:, :].rearrange("p (h d) -> p h d", d=DK), qs[:, par, :, 0, :], s("q_hi"))

            def k_high(n, par):
                reach_alone(pool, s("k_sb"), n + 1, s("pool_passed"))
                split_high(k32[:, par, :].rearrange("p (h d) -> p h d", d=DK), ks[:, par, :, 0, :], s("k_hi"))

            def mask_scores(n, i, g):
                reach_alone(pool, s("sc_odd"), 8 * n + 2 * i + g // 2 + 1, s("pool_passed"))
                pool.affine_select(out=pr_v[:, g, :, :], in_=pr_v[:, g, :, :], compare_op=ALU.is_ge, fill=0.0, base=0,
                                   pattern=[[0, J], [1, P]], channel_multiplier=-1).then_inc(s("pr_odd"), 1)

            def scatter_index(n, c, half):
                if not (isinstance(c, int) and c == 0):
                    pool.wait_ge(s(f"scattered{half}"), 16 * HALF * c)
                pool.tensor_copy(idxq[:, half, :], pos_i[:, bass.ds(c * B + half * HALF, HALF)])\
                    .then_inc(s("idx_ready"), 1)
                reach_alone(pool, s("idx_ready"), n + 1, s("pool_passed"))

            def scatter_rows(i, half):
                pool.indirect_dma_start(slots_d, bass.IndirectOffsetOnAxis(ap=idxq[:, half, i:i + 1], axis=0),
                                        xq[:, half, i, :], None, bounds_check=NS * P - 1, oob_is_err=False)\
                    .then_inc(s(f"scattered{half}"), 16)

            def quad(n, c, half, more):
                for i in range(HALF):
                    mask_scores(n, i, 1)
                    if i == 0:
                        pool.wait_ge(s("xq_ready"), n + 1)
                        scatter_index(n, c, half)
                    scatter_rows(i, half)
                    if more and i == 2:
                        q_high(n + 1, 1 - half)
                        k_high(n + 1, 1 - half)
                    mask_scores(n, i, 3)
                pool.wait_ge(s("ds_sb"), n + 1)
                pool.tensor_tensor(state[:, half * HALF:(half + 1) * HALF, :], state[:, half * HALF:(half + 1) * HALF, :],
                                   dstate[:, :, :], ALU.add).then_inc(s("state_ready"), 1)

            pool.wait_ge(s("b1_ps"), E)
            pool.memset(state[:, :, :], 0.0).then_inc(s("state_zero"), 1)
            pool.wait_ge(s("state_zero"), 1)
            q_high(0, 0)
            k_high(0, 0)
            pool.wait_ge(s("slots_zero"), 16)
            quad(0, 0, 0, True)
            quad(1, 0, 1, True)
            with pool.Fori(1, NCH - 1, 1) as c:
                quad(2 * c, c, 0, True)
                quad(2 * c + 1, c, 1, True)
            quad(NQ - 2, NCH - 1, 0, True)
            quad(NQ - 1, NCH - 1, 1, False)

            for half in range(2):
                pool.wait_ge(s(f"attn_out{half}"), 16 * NCH)

            def gather(k, a):
                reach_alone(pool, s("se_idx"), k + 1, s("pool_passed"))
                pool.indirect_dma_start(att[:, a, :], None, attn_d,
                                        bass.IndirectOffsetOnAxis(ap=idxe[:, a:a + 1].bitcast(U32), axis=0),
                                        bounds_check=NTOK - 1, oob_is_err=False).then_inc(s(f"att_in{a}"), 16)

            def scatter_out(k, a):
                reach_alone(pool, s("ye_ready"), k + 1, s("pool_passed"))
                pool.indirect_dma_start(out_rows, bass.IndirectOffsetOnAxis(ap=idxe[:, a:a + 1].bitcast(U32), axis=0),
                                        ye[:, a, :], None, bounds_check=NTOK - 1, oob_is_err=False)\
                    .then_inc(s(f"out_done{a}"), 16)

            gather(0, 0)
            gather(1, 1)
            with pool.Fori(0, NS // 4 - 1, 1) as i:
                for a in range(4):
                    gather(4 * i + a + 2, (a + 2) % 4)
                    scatter_out(4 * i + a, a)
            for k in range(NS - 4, NS):
                if k + 2 < NS:
                    gather(k + 2, (k + 2) % 4)
                scatter_out(k, k % 4)

        @block.scalar
        def _(act):
            act.dma_start(cen_t[:, :], centroids.rearrange("e d -> d e"), allow_slow_non_contiguous=True).then_inc(s("cen_in"), 16)
            act.dma_start(g_t[:, :], ln_g.rearrange("e d -> d e"), allow_slow_non_contiguous=True).then_inc(s("lng_in"), 16)
            act.dma_start(lb_t[:, :], ln_b.rearrange("e d -> d e"), allow_slow_non_contiguous=True).then_inc(s("lng_in"), 16)
            act.wait_ge(s("eps_ready"), 1)

            def ln_chunk(c, a):
                act.wait_ge(s("mv_ready"), c + 1)
                nc.scalar.activation(std[:, a, :], mv[:, a, :, 1], ACT.Sqrt, bias=eps[:, 0:1]).then_inc(s("std_ready"), 1)
                for hf in range(2):
                    act.wait_ge(s("xta_ps"), 2 * c + hf + 1)
                    reach(act, s("aff_ps"), 2 * c + hf - 1)
                    nc.scalar.activation(xta[:, hf, :, :], banks[hf][:, :].rearrange("p (a b) -> p a b", a=HALF),
                                         ACT.Copy).then_inc(s("xta_sb"), 1)
                act.wait_ge(s("lnx_ready"), c + 1)
                nc.scalar.activation(rows[:, bass.ds(c * B, B), 0:D], lnx[:, a, :, :], ACT.Copy)\
                    .then_inc(s("rows_ready"), 1)

            ln_chunk(0, 0)
            ln_chunk(1, 1)
            with act.Fori(1, NCH // 2, 1) as i:
                for a in range(2):
                    ln_chunk(2 * i + a, a)

            act.wait_ge(s("var2_ready"), 1)
            nc.scalar.activation(tmp_nt2[:, :], tmp_nt[:, :], ACT.Sqrt, bias=eps[:, 0:1]).then_inc(s("std2_ready"), 1)

            def prep(e, a):
                act.wait_ge(s("lng_in"), 32)
                act.wait_ge(s("w1t_ps"), e + 1)
                reach(act, s("b1_ps"), e)
                nc.scalar.activation(w1tr, banks[2][:, :], ACT.Copy)
                nc.scalar.activation(lbb, ones[:, :], ACT.Copy, scale=lb_t[:, bass.ds(e, 1)]).then_inc(s("w1tr_ready"), 1)
                nc.scalar.activation(w1t[:, e, :], banks[2][:, :], ACT.Copy, scale=g_t[:, bass.ds(e, 1)])\
                    .then_inc(s("w1t_ready"), 1)
                act.wait_ge(s("w2t_ps"), e + 1)
                nc.scalar.activation(w2t[:, e, :, :], banks[3][:, :].rearrange("p (c d) -> p c d", c=FC), ACT.Copy)\
                    .then_inc(s("w2t_ready"), 1)
                act.wait_ge(s("b1_ps"), e + 1)
                nc.scalar.activation(b1b[:, e, :], banks[4][:, :], ACT.Copy).then_inc(s("b1b_ready"), 1)

            prep(0, 0)
            prep(1, 1)
            with act.Fori(1, E // 2, 1) as i:
                prep(2 * i, 0)
                prep(2 * i + 1, 1)

            act.wait_ge(s("mx_ready"), 1)
            nc.scalar.activation(rows[:, :, D + 1], mx[:, :], ACT.Sigmoid).then_inc(s("gate_ready"), 1)

            act.wait_ge(s("qbound"), 1)
            nc.scalar.activation(tmp_nt[:, 0:H], tmp_nt2[:, 0:H], ACT.Sqrt, scale=float(P) / (QTOP * QTOP))\
                .then_inc(s("qbound_root"), 1)

            def x_transposed(n):
                act.wait_ge(s("xt_ps"), n + 1)
                reach(act, s("v_ps"), n)
                nc.scalar.activation(xt[:, :, :].rearrange("p a b -> p (a b)"), EB[:, :], ACT.Copy).then_inc(s("xt_sb"), 1)

            def q_copy(n):
                act.wait_ge(s("q_ps"), n + 1)
                reach(act, s("q_lo"), n)
                reach(act, s("qt_ps"), n)
                nc.scalar.activation(q32[:, :], CB[:, :], ACT.Copy).then_inc(s("q_sb"), 1)

            def k_square(n):
                act.wait_ge(s("k_ps"), n + 1)
                reach(act, s("kvar_ready"), n)
                nc.scalar.activation(sq[:, :], EB[:, :], ACT.Square).then_inc(s("sq_ready"), 1)

            def k_root(n):
                act.wait_ge(s("kvar_ready"), n + 1)
                reach(act, s("k_sb"), n)
                nc.scalar.activation(kstd[:, :], kvar[:, :], ACT.Sqrt, scale=1.0 / DK, bias=eps[:, 0:1])\
                    .then_inc(s("kstd_ready"), 1)

            def v_copy(n, par):
                act.wait_ge(s("v_ps"), n + 1)
                reach(act, s("ds_ps"), n - 1)
                nc.scalar.activation(v32[:, par, :], CB[:, :], ACT.Copy).then_inc(s("v_sb"), 1)

            def q_transposed(n):
                act.wait_ge(s("qt_ps"), n + 1)
                reach(act, s("in_ps"), n)
                nc.scalar.activation(qt[:, :, :].rearrange("p a b -> p (a b)"), EB[:, :], ACT.Copy).then_inc(s("qt_sb"), 1)

            def qq_copy(m, a):
                act.wait_ge(s("qk_ps"), m + 1)
                reach(act, s("sc_ps"), 4 * (m - 1))
                nc.scalar.activation(qqt[:, a, :, :], qb16, ACT.Copy).then_inc(s("qq_sb"), 1)

            def score_copy(m, g):
                act.wait_ge(s("sc_ps"), 4 * m + g + 1)
                reach(act, s("av_ps"), 4 * (m - 1) + g + 1)
                nc.scalar.activation(pr[:, g, :], SC[1][:, :], ACT.Copy).then_inc(s("sc_odd"), 1)

            def y_copy(m, a):
                act.wait_ge(s("av_ps"), 4 * m + 4)
                reach(act, s("out_ps"), m - 1)
                nc.scalar.activation(ys[:, a, :, :].rearrange("p j t -> p (j t)"), YB[:, :], ACT.Copy).then_inc(s("y_sb"), 1)

            def quad(n, c, half, more):
                for i in range(HALF):
                    m = 4 * n + i
                    score_copy(m, 1)
                    if more and i == 0:
                        x_transposed(n + 1)
                    if more and i == 1:
                        q_copy(n + 1)
                        k_square(n + 1)
                    if more and i == 2:
                        k_root(n + 1)
                    score_copy(m, 3)
                    if more and i == 2:
                        v_copy(n + 1, 1 - half)
                    if more and i == 3:
                        q_transposed(n + 1)
                    if more or i < 3:
                        qq_copy(m + 1, (i + 1) % 2)
                    y_copy(m, i % 2)

            act.wait_ge(s("b1b_ready"), E)
            x_transposed(0)
            q_copy(0)
            k_square(0)
            k_root(0)
            v_copy(0, 0)
            q_transposed(0)
            qq_copy(0, 0)
            quad(0, 0, 0, True)
            quad(1, 0, 1, True)
            with act.Fori(1, NCH - 1, 1) as c:
                quad(2 * c, c, 0, True)
                quad(2 * c + 1, c, 1, True)
            quad(NQ - 2, NCH - 1, 0, True)
            quad(NQ - 1, NCH - 1, 1, False)

            def se_x(k, a):
                act.wait_ge(s("sex_ps"), k + 1)
                reach(act, s("h_ps"), k - 1)
                nc.scalar.activation(xse[:, a % 2, :], banks[6 + a % 2][:, 0:P], ACT.Copy).then_inc(s("sex_sb"), 1)

            def se_relu(k, a):
                act.wait_ge(s("ht_ps"), k + 1)
                reach(act, s("ye_ps"), k - 1)
                nc.scalar.activation(ht[:, a % 2, :], banks[2 + a % 2][:, :], ACT.Relu).then_inc(s("ht_sb"), 1)

            se_x(0, 0)
            se_x(1, 1)
            for k in range(2):
                se_relu(k, k)
                se_x(k + 2, k)
            with act.Fori(1, NS // 2 - 1, 1) as i:
                for a in range(2):
                    se_relu(2 * i + a, a)
                    se_x(2 * i + a + 2, a)
            for a in range(2):
                se_relu(NS - 2 + a, a)

        @block.vector
        def _(dve):
            chain = [0]

            def link(ins):
                chain[0] += 1
                ins.then_inc(s("dve_chain"), 1)
                dve.wait_ge(s("dve_chain"), chain[0])

            nc.vector.memset(eps[:, :], EPS).then_inc(s("eps_ready"), 1)
            nc.vector.memset(ones[:, :], 1.0).then_inc(s("ones_ready"), 1)
            nc.vector.memset(onesb[:, :], 1.0)
            for e in range(E):
                nc.vector.memset(desc[:, e:e + 1], float(E - e))

            def ln_chunk(i, a):
                c = 2 * i + a
                dve.wait_ge(s(f"x_in{a}"), 16 * (i + 1))
                for b in range(B):
                    last = nc.vector.bn_stats(stats[:, a, b, :], resid[:, c * B + b, :])
                last.then_inc(s("stats_done"), 1)
                reach_alone(dve, s("stats_done"), c + 1, s("dve_passed"))
                for b in range(B):
                    last = nc.vector.bn_aggr(mv[:, a, b, :], stats[:, a, b, :])
                last.then_inc(s("mv_ready"), 1)
                dve.wait_ge(s("mv_ready"), c + 1)
                nc.vector.tensor_copy(var_all[:, bass.ds(c * B, B)], mv[:, a, :, 1])
                dve.wait_ge(s("std_ready"), c + 1)
                nc.vector.reciprocal(rs_s[:, a, :], std[:, a, :]).then_inc(s("rs_done"), 1)
                dve.wait_ge(s("rs_done"), c + 1)
                nc.vector.tensor_copy(rstd_all[:, bass.ds(c * B, B)], rs_s[:, a, :])
                reach(dve, s("xta_ps"), 2 * (c - 1))
                reach(dve, s("resid_ready"), c - 1)
                reach(dve, s("rows_ready"), c - 1)
                for b in range(B):
                    last = nc.vector.tensor_scalar(lnx[:, a, b, :], resid[:, c * B + b, :], mv[:, a, b, 0:1],
                                                   rs_s[:, a, b:b + 1], ALU.subtract, ALU.mult)
                last.then_inc(s("lnx_ready"), 1)

            ln_chunk(0, 0)
            ln_chunk(0, 1)
            with dve.Fori(1, NCH // 2, 1) as i:
                for a in range(2):
                    ln_chunk(i, a)

            dve.wait_ge(s("lnx_ready"), NCH)
            link(nc.vector.tensor_tensor(tmp_nt[:, :], rstd_all[:, :], rstd_all[:, :], ALU.mult))
            nc.vector.tensor_tensor(tmp_nt[:, :], tmp_nt[:, :], var_all[:, :], ALU.mult).then_inc(s("var2_ready"), 1)

            dve.wait_ge(s("aff_ps"), 2 * NCH)
            dve.wait_ge(s("pool_m"), 8)
            nc.vector.tensor_copy(before[:, :], rt1.rearrange("p t e -> p (t e)")[:, 0:P])
            link(nc.vector.tensor_copy(jmask[:, :], rt1.rearrange("p t e -> p (t e)")[:, P:P + J]))
            for g in range(1, G):
                link(nc.vector.tensor_tensor(jmask[:, :], jmask[:, :],
                                             rt1.rearrange("p t e -> p (t e)")[:, P + J * g:P + J * (g + 1)], ALU.add))
            nc.vector.tensor_copy(iotk[:, :], iot_i[:, :])
            link(nc.vector.tensor_copy(aff, banks[7][:, :].rearrange("p (t e) -> p t e", e=E)))

            def over_e(v):
                return bcast(v, 2, E)

            def over_t(v, n=NT):
                return bcast(v, 1, n)

            nc.vector.tensor_reduce(out=mx[:, :], in_=aff, axis=AX, op=ALU.max).then_inc(s("mx_ready"), 1)
            dve.wait_ge(s("mx_ready"), 1)
            link(nc.vector.tensor_tensor(rt2, aff, over_e(mx[:, :]), ALU.is_ge))
            link(nc.vector.tensor_tensor(rt2, rt2, over_t(desc[:, :]), ALU.mult))
            link(nc.vector.tensor_reduce(out=rstd_all[:, :], in_=rt2, axis=AX, op=ALU.max))
            nc.vector.tensor_tensor(ohb[:, :, :], rt2, over_e(rstd_all[:, :]), ALU.is_equal).then_inc(s("oh_ready"), 1)
            dve.wait_ge(s("std2_ready"), 1)
            link(nc.vector.reciprocal(rows[:, :, D], tmp_nt2[:, :]))
            nc.vector.tensor_copy(rows[:, :, D + 2], id_i[:, :])
            nc.vector.memset(rows[:, :, D + 3], 0.0)
            dve.wait_ge(s("rank_ps"), 2)
            link(nc.vector.tensor_copy(rt3, banks[6][:, :].rearrange("p (t e) -> p t e", e=E)))
            nc.vector.tensor_copy(rt1, rt3)
            cur, nxt = rt3, rt4
            step = 1
            while step < NT:
                nc.vector.tensor_copy(nxt[:, 0:step, :], cur[:, 0:step, :])
                link(nc.vector.tensor_tensor(nxt[:, step:NT, :], cur[:, step:NT, :], cur[:, 0:NT - step, :], ALU.add))
                cur, nxt = nxt, cur
                step *= 2
            tiles_cmp = aff.rearrange("p t e -> p (t e)").rearrange("p (e k) -> p e k", e=E)
            link(nc.vector.tensor_scalar(cnt[:, 0, :], cur[:, NT - 1, :], 1.0 / P, None, ALU.mult))
            link(nc.vector.tensor_tensor(tiles_cmp, bcast(cnt[:, 0, :], 2, NT),
                                         over_t(iotk[:, 0:NT], E), ALU.is_gt))
            link(nc.vector.tensor_reduce(out=cnt[:, 1, :], in_=tiles_cmp, axis=AX, op=ALU.add))
            link(nc.vector.tensor_copy(cnt[:, 2, :], cnt[:, 1, :]))
            a_, b_ = 2, 3
            step = 1
            while step < E:
                nc.vector.tensor_copy(cnt[:, b_, 0:step], cnt[:, a_, 0:step])
                link(nc.vector.tensor_tensor(cnt[:, b_, step:E], cnt[:, a_, step:E], cnt[:, a_, 0:E - step], ALU.add))
                a_, b_ = b_, a_
                step *= 2
            dve.wait_ge(s("rows_ready"), NCH)
            dve.wait_ge(s("resid_ready"), NCH)
            link(nc.vector.tensor_tensor(eidf, over_t(cnt[:, a_, :], NS),
                                         bcast(iotk[:, :], 2, E), ALU.is_le))
            link(nc.vector.tensor_reduce(out=iotk[:, :], in_=eidf, axis=AX, op=ALU.add))
            nc.vector.tensor_scalar(eid_i[:, :], iotk[:, :], float(E - 1), None, ALU.min).then_inc(s("eid_ready"), 1)
            link(nc.vector.tensor_tensor(cnt[:, 4, :], cnt[:, a_, :], cnt[:, 1, :], ALU.subtract))
            link(nc.vector.tensor_scalar(cnt[:, 4, :], cnt[:, 4, :], float(P), None, ALU.mult))
            link(nc.vector.tensor_tensor(cur, cur, rt1, ALU.subtract))
            link(nc.vector.tensor_tensor(cur, cur, over_t(cnt[:, 4, :]), ALU.add))
            link(nc.vector.tensor_tensor(cur, banks[5][:, :].rearrange("p (t e) -> p t e", e=E), cur, ALU.add))
            link(nc.vector.tensor_tensor(cur, cur, ohb[:, :, :], ALU.mult))
            link(nc.vector.tensor_reduce(out=tmp_nt[:, :], in_=cur, axis=AX, op=ALU.add))
            nc.vector.tensor_copy(pos_i[:, :], tmp_nt[:, :]).then_inc(s("route_done"), 1)

            dve.wait_ge(s("wqkv_in"), 16)
            for part in range(2):
                nc.vector.tensor_copy(wqkv[:, part * D:(part + 1) * D].rearrange("p (j g d) -> p j g d", j=J, g=G),
                                      wraw[:, part * D:(part + 1) * D].rearrange("p (g j d) -> p j g d", j=J, g=G))
            link(nc.vector.tensor_copy(wqkv[:, 2 * D:3 * D], wraw[:, 2 * D:3 * D]))
            wk = wqkv[:, D:2 * D].rearrange("p (h d) -> p h d", d=DK)
            link(nc.vector.tensor_reduce(out=tmp_nt[:, 0:H], in_=wk, axis=AX, op=ALU.add))
            link(nc.vector.tensor_scalar(tmp_nt[:, 0:H], tmp_nt[:, 0:H], 1.0 / DK, None, ALU.mult))
            nc.vector.tensor_tensor(wk, wk, bcast(tmp_nt[:, 0:H], 2, DK),
                                    ALU.subtract)
            nc.vector.tensor_tensor(sq[:, 0:D], wqkv[:, 0:D], wqkv[:, 0:D], ALU.mult).then_inc(s("wq_sq"), 1)
            dve.wait_ge(s("norm_ps"), 1)
            nc.vector.tensor_reduce(out=tmp_nt2[:, 0:H], in_=banks[6][:, 0:D].rearrange("p (h d) -> p h d", d=DK),
                                    axis=AX, op=ALU.max).then_inc(s("qbound"), 1)
            dve.wait_ge(s("qbound_root"), 1)
            link(nc.vector.tensor_scalar(tmp_nt[:, 0:H], tmp_nt[:, 0:H], TINY, None, ALU.max))
            link(nc.vector.reciprocal(tmp_nt[:, H:2 * H], tmp_nt[:, 0:H]))
            wq = wqkv[:, 0:D].rearrange("p (h d) -> p h d", d=DK)
            nc.vector.tensor_tensor(wq, wq, bcast(tmp_nt[:, H:2 * H], 2, DK),
                                    ALU.mult).then_inc(s("wqkv_ready"), 1)
            dve.wait_ge(s("ident_ready"), 1)
            dve.wait_ge(s("wo_in"), 16)
            bound = tmp_nt[:, 0:H]
            per = sq[:, D:2 * D].rearrange("p (h d) -> p h d", d=DK)
            idv = ident[:, :].rearrange("p (h d) -> p h d", d=DK)
            for g in range(G):
                last = nc.vector.tensor_tensor(per[:, J * g:J * (g + 1), :], idv[:, J * g:J * (g + 1), :],
                                               bcast(bound[:, g:H:G], 2, DK), ALU.mult)
            link(last)
            link(nc.vector.tensor_reduce(out=cnt[:, 0, 0:1], in_=sq[:, D:2 * D], axis=AX, op=ALU.add))
            link(nc.vector.tensor_scalar(wo[:, :], wo[:, :], cnt[:, 0, 0:1], None, ALU.mult))
            for j in range(J):
                last = nc.vector.tensor_scalar(wom[:, j, :], wo[:, :], jmask[:, j:j + 1], None, ALU.mult)
            nc.vector.tensor_copy(identh[:, :], ident[:, :])
            nc.vector.memset(att[:, :, :], 0.0).then_inc(s("wo_ready"), 1)

            def x_copy(n, c, half):
                reach(dve, s("xt_ps"), n - 1)
                if not (isinstance(c, int) and c == 0):
                    dve.wait_ge(s(f"scattered{half}"), 16 * HALF * c)
                nc.vector.tensor_copy(xq[:, half, :, :], rows[:, bass.ds(c * B + half * HALF, HALF), :])\
                    .then_inc(s("xq_ready"), 1)

            def k_var(n):
                dve.wait_ge(s("sq_ready"), n + 1)
                nc.vector.tensor_reduce(out=kvar[:, :], in_=sq[:, :].rearrange("p (h d) -> p h d", d=DK), axis=AX,
                                        op=ALU.add).then_inc(s("kvar_ready"), 1)

            def k_norm(n, par):
                dve.wait_ge(s("kstd_ready"), n + 1)
                nc.vector.reciprocal(krs[:, :], kstd[:, :]).then_inc(s("krs_ready"), 1)
                dve.wait_ge(s("krs_ready"), n + 1)
                reach(dve, s("ds_ps"), n - 1)
                nc.vector.tensor_tensor(k32[:, par, :].rearrange("p (h d) -> p h d", d=DK),
                                        EB[:, :].rearrange("p (h d) -> p h d", d=DK),
                                        bcast(krs[:, :], 2, DK), ALU.mult)\
                    .then_inc(s("k_sb"), 1)

            def q_low(n, par):
                dve.wait_ge(s("q_hi"), n + 1)
                nc.vector.tensor_tensor(qs[:, par, :, 2, :], q32[:, :].rearrange("p (h d) -> p h d", d=DK),
                                        qs[:, par, :, 0, :], ALU.subtract).then_inc(s("q_lo"), 1)
                dve.wait_ge(s("q_lo"), n + 1)
                nc.vector.tensor_copy(qs[:, par, :, 1::2, :], qs[:, par, :, 0::2, :]).then_inc(s("q_parts"), 1)

            def k_low(n, par):
                dve.wait_ge(s("k_hi"), n + 1)
                nc.vector.tensor_tensor(ks[:, par, :, 1, :], k32[:, par, :].rearrange("p (h d) -> p h d", d=DK),
                                        ks[:, par, :, 0, :], ALU.subtract).then_inc(s("k_lo"), 1)
                dve.wait_ge(s("k_lo"), n + 1)
                nc.vector.tensor_copy(ks[:, par, :, 2:4, :], ks[:, par, :, 0:2, :]).then_inc(s("k_parts"), 1)

            def kk_copy(m, a):
                dve.wait_ge(s("qk_ps"), m + 1)
                reach(dve, s("sc_ps"), 4 * (m - 1))
                nc.vector.tensor_copy(kkt[:, a, :, :], kb16).then_inc(s("kk_sb"), 1)

            def score_mask(m, g):
                dve.wait_ge(s("sc_ps"), 4 * m + g + 1)
                reach(dve, s("av_ps"), 4 * (m - 1) + g + 1)
                nc.vector.tensor_tensor(pr_v[:, g, :, :], SC[0][:, :].rearrange("p (j t) -> p j t", j=J),
                                        bcast(causal[:, :], 1, J), ALU.mult)\
                    .then_inc(s("pr_even"), 1)

            def inter_copy(n):
                dve.wait_ge(s("in_ps"), n + 1)
                reach(dve, s("out_ps"), 4 * n)
                nc.vector.tensor_copy(yint[:, :, :].rearrange("p a b -> p (a b)"), EB[:, :]).then_inc(s("yi_sb"), 1)

            def dstate_mask(n):
                dve.wait_ge(s("ds_ps"), n + 1)
                reach(dve, s("state_ready"), n)
                nc.vector.tensor_tensor(dstate[:, :, :], CB[:, :].rearrange("p (a b) -> p a b", a=HALF),
                                        bcast(headmask[:, :], 1, HALF), ALU.mult)\
                    .then_inc(s("ds_sb"), 1)

            def result(n, c, half):
                dve.wait_ge(s("out_ps"), 4 * n + 4)
                if not (isinstance(c, int) and c == 0):
                    dve.wait_ge(s(f"attn_out{half}"), 16 * c)
                nc.vector.tensor_tensor(res[:, half, :, :], DB[:, :].rearrange("p (a b) -> p a b", a=HALF),
                                        resid[:, bass.ds(c * B + half * HALF, HALF), :], ALU.add)\
                    .then_inc(s("res_ready"), 1)

            def quad(n, c, half, more):
                for i in range(HALF):
                    m = 4 * n + i
                    score_mask(m, 0)
                    if i == 0:
                        if more:
                            x_copy(n + 1, c if half == 0 else c + 1, 1 - half)
                        inter_copy(n)
                    if more and i == 2:
                        k_norm(n + 1, 1 - half)
                    score_mask(m, 2)
                    if more and i == 1:
                        k_var(n + 1)
                    if more and i == 2:
                        q_low(n + 1, 1 - half)
                    if more and i == 3:
                        k_low(n + 1, 1 - half)
                    if more or i < 3:
                        kk_copy(m + 1, (i + 1) % 2)
                dstate_mask(n)
                result(n, c, half)

            dve.wait_ge(s("gate_ready"), 1)
            dve.wait_ge(s("rows_ready"), NCH)
            dve.wait_ge(s("resid_ready"), NCH)
            x_copy(0, 0, 0)
            k_var(0)
            k_norm(0, 0)
            q_low(0, 0)
            k_low(0, 0)
            kk_copy(0, 0)
            quad(0, 0, 0, True)
            quad(1, 0, 1, True)
            with dve.Fori(1, NCH - 1, 1) as c:
                quad(2 * c, c, 0, True)
                quad(2 * c + 1, c, 1, True)
            quad(NQ - 2, NCH - 1, 0, True)
            quad(NQ - 1, NCH - 1, 1, False)

            dve.wait_ge(s("eid_ready"), 1)
            dve.wait_ge(s("b2_in"), 16)
            dve.wait_ge(s("b1b_ready"), E)

            def se_index(k, a, rnd):
                dve.wait_ge(s(f"se_in{a}"), 16 * (rnd + 1))
                reach(dve, s(f"out_done{a}"), 16 * rnd)
                nc.vector.tensor_scalar(idxe[:, a:a + 1], xs[:, a, D + 2:D + 3], -1.0, float(NTOK), ALU.mult, ALU.add)\
                    .then_inc(s("se_idx"), 1)

            def se_bias(k, a):
                e = dve.value_load(eid_i[0:1, bass.ds(k, 1)], min_val=0, max_val=E - 1)
                dve.wait_ge(s("h_ps"), k + 1)
                reach(dve, s("ht_ps"), k - 1)
                nc.vector.scalar_tensor_tensor(out=hb[:, a % 2, :], in0=banks[a % 2][:, :], scalar=xs[:, a, D:D + 1],
                                               in1=b1b[:, e, :], op0=ALU.mult, op1=ALU.add).then_inc(s("hb_ready"), 1)

            def se_result(k, a, rnd):
                e = dve.value_load(eid_i[0:1, bass.ds(k, 1)], min_val=0, max_val=E - 1)
                dve.wait_ge(s("ye_ps"), k + 1)
                nc.vector.tensor_tensor(yb[:, a % 2, :], banks[4 + a % 2][:, 0:D], b2b[:, e, :], ALU.add)\
                    .then_inc(s("yb_done"), 1)
                dve.wait_ge(s(f"att_in{a}"), 16 * (rnd + 1))
                dve.wait_ge(s("yb_done"), k + 1)
                nc.vector.scalar_tensor_tensor(out=ye[:, a, :], in0=yb[:, a % 2, :], scalar=xs[:, a, D + 1:D + 2],
                                               in1=att[:, a, :], op0=ALU.mult, op1=ALU.add).then_inc(s("ye_ready"), 1)

            def expert_round(i, last=False):
                for a in range(4):
                    k = 4 * i + a
                    se_bias(k, a)
                    if a > 0:
                        se_result(k - 1, a - 1, i)
                    elif not (isinstance(i, int) and i == 0):
                        se_result(k - 1, 3, i - 1)
                    if not last or a < 2:
                        se_index(k + 2, (a + 2) % 4, i + (a + 2) // 4)

            se_index(0, 0, 0)
            se_index(1, 1, 0)
            expert_round(0)
            with dve.Fori(1, NS // 4 - 1, 1) as i:
                expert_round(i)
            expert_round(NS // 4 - 1, last=True)
            se_result(NS - 1, 3, NS // 4 - 1)

        @block.tensor
        def _(pe):
            mm = nc.tensor.matmul
            pe.wait_ge(s("ident_ready"), 1)
            pe.wait_ge(s("cen_in"), 16)

            def ln_chunk(c, a):
                pe.wait_ge(s("lnx_ready"), c + 1)
                for hf in range(2):
                    reach(pe, s("xta_sb"), 2 * (c - 1) + hf + 1)
                    for b in range(HALF):
                        last = nc.tensor.transpose(banks[hf][:, b * P:(b + 1) * P], lnx[:, a, hf * HALF + b, :], ident[:, :])
                    last.then_inc(s("xta_ps"), 1)
                for hf in range(2):
                    pe.wait_ge(s("xta_sb"), 2 * c + hf + 1)
                    for b in range(HALF):
                        last = mm(banks[7][:, bass.ds((c * B + hf * HALF + b) * E, E)], xta[:, hf, b, :], cen_t[:, :],
                                  start=True, stop=True)
                    last.then_inc(s("aff_ps"), 1)

            ln_chunk(0, 0)
            ln_chunk(1, 1)
            with pe.Fori(1, NCH // 2, 1) as i:
                for a in range(2):
                    ln_chunk(2 * i + a, a)

            pe.wait_ge(s("ones_ready"), 1)

            def prep(e, a, i):
                pe.wait_ge(s(f"wraw_in{a}"), 48 * (i + 1))
                reach(pe, s("w1t_ready"), e)
                for c in range(FC):
                    last = nc.tensor.transpose(banks[2][:, c * P:(c + 1) * P], w1raw[:, a, c, :], ident[:, :])
                last.then_inc(s("w1t_ps"), 1)
                reach(pe, s("w2t_ready"), e)
                for c in range(FC):
                    last = nc.tensor.transpose(banks[3][:, c * P:(c + 1) * P], w2raw[:, a, c * P:(c + 1) * P], ident[:, :])
                last.then_inc(s("w2t_ps"), 1)
                pe.wait_ge(s("w1tr_ready"), e + 1)
                reach(pe, s("b1b_ready"), e)
                mm(banks[4][:, :], lbb, w1tr, start=True, stop=False)
                mm(banks[4][:, :], ones[0:1, :], b1row[a], start=False, stop=True).then_inc(s("b1_ps"), 1)

            prep(0, 0, 0)
            prep(1, 1, 0)
            with pe.Fori(1, E // 2, 1) as i:
                for a in range(2):
                    prep(2 * i + a, a, i)

            pe.wait_ge(s("oh_ready"), 1)
            ohv = ohb[:, :, :].rearrange("p t e -> p (t e)")
            mm(banks[5][:, :], before[:, :], ohv, start=True, stop=True).then_inc(s("rank_ps"), 1)
            mm(banks[6][:, :], onesb[:, :], ohv, start=True, stop=True).then_inc(s("rank_ps"), 1)

            pe.wait_ge(s("wq_sq"), 1)
            mm(banks[6][:, 0:D], ones[:, :], sq[:, 0:D], start=True, stop=True).then_inc(s("norm_ps"), 1)

            def x_trans(n, par):
                pe.wait_ge(s("xq_ready"), n + 1)
                reach(pe, s("yi_sb"), n)
                for i in range(HALF):
                    last = nc.tensor.transpose(EB[:, i * P:(i + 1) * P], xq[:, par, i, 0:D], ident[:, :])
                last.then_inc(s("xt_ps"), 1)

            def project(bank, col, done):
                for i in range(HALF):
                    last = mm(bank[:, i * P:(i + 1) * P], xt[:, i, :], wqkv[:, col:col + D], start=True, stop=True)
                last.then_inc(s(done), 1)

            def q_project(n):
                pe.wait_ge(s("xt_sb"), n + 1)
                reach(pe, s("ds_sb"), n - 1)
                project(CB, 0, "q_ps")

            def k_project(n):
                project(EB, D, "k_ps")

            def v_project(n):
                pe.wait_ge(s("q_sb"), n + 1)
                project(CB, 2 * D, "v_ps")

            def q_trans(n):
                pe.wait_ge(s("k_sb"), n + 1)
                for i in range(HALF):
                    last = nc.tensor.transpose(EB[:, i * P:(i + 1) * P], q32[:, i * D:(i + 1) * D], ident[:, :])
                last.then_inc(s("qt_ps"), 1)

            def qk_trans(m, n, i, par):
                if i == 0:
                    pe.wait_ge(s("q_parts"), n + 1)
                    pe.wait_ge(s("k_parts"), n + 1)
                reach(pe, s("qq_sb"), m)
                reach(pe, s("kk_sb"), m)
                for j in range(J):
                    h0 = i * H + j * G
                    qv = qs[:, par, h0:h0 + G, :, :].rearrange("p g r d -> p (g r d)")
                    nc.tensor.transpose(qb16[:, j, :], qv, identh[:, :])
                    kv = ks[:, par, h0:h0 + G, :, :].rearrange("p g r d -> p (g r d)")
                    last = nc.tensor.transpose(kb16[:, j, :], kv, identh[:, :])
                last.then_inc(s("qk_ps"), 1)

            def scores(m, i, g):
                if g == 0:
                    pe.wait_ge(s("qq_sb"), m + 1)
                    pe.wait_ge(s("kk_sb"), m + 1)
                reach(pe, s("sc_odd" if g % 2 else "pr_even"), 2 * m + g // 2)
                for j in range(J):
                    last = mm(SC[g % 2][:, j * P:(j + 1) * P], kkt[32 * g:32 * (g + 1), i % 2, j, :],
                              qqt[32 * g:32 * (g + 1), i % 2, j, :], start=True, stop=True)
                last.then_inc(s("sc_ps"), 1)

            def weighted(m, i, par, g):
                if g == 0:
                    reach(pe, s("y_sb"), m)
                pe.wait_ge(s("pr_odd" if g % 2 else "pr_even"), 2 * m + g // 2 + 1)
                mm(YB[32 * g:32 * (g + 1), :], v32[:, par, i * D + 32 * g:i * D + 32 * (g + 1)], pr[:, g, :], start=True, stop=True).then_inc(s("av_ps"), 1)

            def output(m, n, i):
                if i == 0:
                    reach(pe, s("res_ready"), n)
                    pe.wait_ge(s("yi_sb"), n + 1)
                pe.wait_ge(s("y_sb"), m + 1)
                o = DB[:, i * D:(i + 1) * D]
                mm(o, yint[:, i, :], wo[:, :], start=True, stop=False)
                for j in range(J):
                    last = mm(o, ys[:, i % 2, j, :], wom[:, j, :], start=False, stop=(j == J - 1))
                last.then_inc(s("out_ps"), 1)

            def inter(n, half):
                pe.wait_ge(s("qt_sb"), n + 1)
                reach(pe, s("state_ready"), n - 1)
                for i in range(HALF):
                    last = mm(EB[:, i * P:(i + 1) * P], state[:, half * HALF + i, :], qt[:, i, :], start=True, stop=True)
                last.then_inc(s("in_ps"), 1)

            def state_step(n, par, more):
                pe.wait_ge(s("v_sb"), n + 2 if more else n + 1)
                for i in range(HALF):
                    last = mm(CB[:, i * P:(i + 1) * P], k32[:, par, i * D:(i + 1) * D], v32[:, par, i * D:(i + 1) * D],
                              start=True, stop=True)
                last.then_inc(s("ds_ps"), 1)

            def quad(n, c, half, more):
                for i in range(HALF):
                    m = 4 * n + i
                    scores(m, i, 0)
                    scores(m, i, 1)
                    if i == 0:
                        inter(n, half)
                    else:
                        output(m - 1, n, i - 1)
                    weighted(m, i, half, 0)
                    scores(m, i, 2)
                    weighted(m, i, half, 1)
                    scores(m, i, 3)
                    if more and i == 0:
                        x_trans(n + 1, 1 - half)
                    if more and i == 1:
                        q_project(n + 1)
                        k_project(n + 1)
                    if more and i == 2:
                        v_project(n + 1)
                    if more and i == 3:
                        q_trans(n + 1)
                    weighted(m, i, half, 2)
                    if i < 3:
                        qk_trans(m + 1, n, i + 1, half)
                    elif more:
                        qk_trans(m + 1, n + 1, 0, 1 - half)
                    weighted(m, i, half, 3)
                state_step(n, half, more)
                output(4 * n + 3, n, 3)

            pe.wait_ge(s("wqkv_ready"), 1)
            pe.wait_ge(s("wo_ready"), 1)
            pe.wait_ge(s("route_done"), 1)
            pe.wait_ge(s("b1b_ready"), E)
            pe.wait_ge(s("state_zero"), 1)
            x_trans(0, 0)
            q_project(0)
            k_project(0)
            v_project(0)
            q_trans(0)
            qk_trans(0, 0, 0, 0)
            quad(0, 0, 0, True)
            quad(1, 0, 1, True)
            with pe.Fori(1, NCH - 1, 1) as c:
                quad(2 * c, c, 0, True)
                quad(2 * c + 1, c, 1, True)
            quad(NQ - 2, NCH - 1, 0, True)
            quad(NQ - 1, NCH - 1, 1, False)

            pe.wait_ge(s("res_ready"), NQ)
            pe.wait_ge(s("ds_sb"), NQ)
            pe.wait_ge(s("w1t_ready"), E)
            pe.wait_ge(s("w2t_ready"), E)
            pe.wait_ge(s("eid_ready"), 1)

            def se_trans(k, a, rnd):
                pe.wait_ge(s(f"se_in{a}"), 16 * (rnd + 1))
                reach(pe, s("sex_sb"), k - 1)
                nc.tensor.transpose(banks[6 + a % 2][:, 0:P], xs[:, a, 0:D], ident[:, :]).then_inc(s("sex_ps"), 1)

            def se_up(k, a):
                e = pe.value_load(eid_i[0:1, bass.ds(k, 1)], min_val=0, max_val=E - 1)
                pe.wait_ge(s("sex_sb"), k + 1)
                reach(pe, s("hb_ready"), k - 1)
                mm(banks[a % 2][:, :], xse[:, a % 2, :], w1t[:, e, :], start=True, stop=True).then_inc(s("h_ps"), 1)

            def se_hidden(k, a):
                pe.wait_ge(s("hb_ready"), k + 1)
                reach(pe, s("ht_sb"), k - 1)
                for c in range(FC):
                    last = nc.tensor.transpose(banks[2 + a % 2][:, c * P:(c + 1) * P], hb[:, a % 2, c * P:(c + 1) * P],
                                               ident[:, :])
                last.then_inc(s("ht_ps"), 1)

            def se_down(k, a):
                e = pe.value_load(eid_i[0:1, bass.ds(k, 1)], min_val=0, max_val=E - 1)
                pe.wait_ge(s("ht_sb"), k + 1)
                reach(pe, s("yb_done"), k - 1)
                for c in range(FC):
                    last = mm(banks[4 + a % 2][:, 0:D], ht[:, a % 2, c * P:(c + 1) * P], w2t[:, e, c, :],
                              start=(c == 0), stop=(c == FC - 1))
                last.then_inc(s("ye_ps"), 1)

            def expert_round(i, last=False):
                for a in range(4):
                    k = 4 * i + a
                    if not last or a < 3:
                        se_up(k + 1, (a + 1) % 4)
                    se_hidden(k, a)
                    if not (isinstance(i, int) and i == 0 and a == 0):
                        se_down(k - 1, (a - 1) % 4)
                    if not last or a < 2:
                        se_trans(k + 2, (a + 2) % 4, i + (a + 2) // 4)

            se_trans(0, 0, 0)
            se_trans(1, 1, 0)
            se_up(0, 0)
            expert_round(0)
            with pe.Fori(1, NS // 4 - 1, 1) as i:
                expert_round(i)
            expert_round(NS // 4 - 1, last=True)
            se_down(NS - 1, 3)


_INS = ["L0_attn_x", "L0_attn_W_qkv", "L0_attn_W_o", "L0_ffn_centroids", "L0_ffn_ln_g", "L0_ffn_ln_b", "L0_ffn_w1",
        "L0_ffn_b1", "L0_ffn_w2", "L0_ffn_b2"]


def kernel(**inputs):
    import numpy as _np
    import concourse.bacc as _bacc
    from concourse import mybir as _mybir
    from concourse.bass_utils import run_bass_kernel_spmd as _run

    nc = _bacc.Bacc("TRN2", target_bir_lowering=False, num_devices=1)
    arrays, args = {}, []
    for name in _INS:
        a = _np.ascontiguousarray(inputs[name])
        arrays[f"in_{name}_dram"] = a
        args.append(nc.dram_tensor(f"in_{name}_dram", a.shape, _mybir.dt.from_np(a.dtype), kind="ExternalInput").ap())
    args.append(nc.dram_tensor("out_dram", inputs["L0_attn_x"].shape, _mybir.dt.from_np(_np.dtype("float32")),
                               kind="ExternalOutput").ap())
    moe_attention_kernel(nc, *args)
    r = _run(nc, [arrays], core_ids=[0])
    return r.results[0]["out_dram"]
```

```python
import concourse.bass as bass
from concourse import mybir
from contextlib import ExitStack

F32, F16, BF16, I32, U32 = (mybir.dt.float32, mybir.dt.float16, mybir.dt.bfloat16, mybir.dt.int32, mybir.dt.uint32)
ALU = mybir.AluOpType
ACT = mybir.ActivationFunctionType
AX = mybir.AxisListType.X


def reach(eng, sem, value):
    if isinstance(value, int) and value <= 0:
        return
    eng.wait_ge(sem, value)


def reach_alone(eng, sem, value, passed):
    if isinstance(value, int) and value <= 0:
        return
    eng.wait_ge(sem, value)
    if not isinstance(value, int):
        eng.sem_inc(passed, 1)


def moe_attention_kernel(nc, x, w_qkv, w_o, centroids, ln_g, ln_b, w1, b1, w2, b2, out):
    B, L, D = x.shape
    E, F, _ = w1.shape
    P = 128
    H = 16
    DK = D // H
    NCH = L // P
    NT = B * NCH
    NTOK = B * L
    HALF = B // 2
    NQ = NT // HALF
    G = P // 32
    J = H // G
    FC = F // P
    NS = NT + E
    ROW = D + 4
    RING = 8
    ROUNDS = NS // RING
    AHEAD = 4
    EPS = 1e-5
    QTOP = 1024.0
    TINY = 1e-30

    x_v = x.rearrange("b (c p) d -> p c b d", p=P)
    slots_d = nc.dram_tensor("slots_d", (NS * P, ROW), F32, kind="Internal").ap()
    attn_d = nc.dram_tensor("attn_d", (NTOK, D), F32, kind="Internal").ap()
    attn_v = attn_d.rearrange("(b c p) d -> p c b d", p=P, c=NCH)
    slots_v = slots_d.rearrange("(k p) r -> p k r", p=P)
    out_rows = out.rearrange("b l d -> (b l) d")

    ctx = ExitStack()
    with ctx:
        def sb(name, shape, dt=F32):
            return ctx.enter_context(nc.sbuf_tensor(name, shape, dt))

        def sem(name):
            return ctx.enter_context(nc.semaphore(name))

        resid = sb("resid", [P, NT, D])
        rows = sb("rows", [P, NT, ROW])
        w1t = sb("w1t", [P, E, F])
        b1b = sb("b1b", [P, E, F])
        w2t = sb("w2t", [P, E, FC, D])
        b2b = sb("b2b", [P, E, D])
        pos_i = sb("pos_i", [P, NT], I32)
        eid_i = sb("eid_i", [P, NS + RING], I32)
        wqkv = sb("wqkv", [P, 3 * D])
        wo = sb("wo", [P, D])
        wom = sb("wom", [P, J, D])
        ident = sb("ident", [P, P])
        identh = sb("identh", [P, P], F16)
        causal = sb("causal", [P, P])
        headmask = sb("headmask", [P, P])
        jmask = sb("jmask", [P, J])
        eps = sb("eps", [P, 1])
        ones = sb("ones", [P, P])
        zrow = sb("zrow", [P, ROW])

        stats = sb("stats", [P, 2, B, 6])
        mv = sb("mv", [P, 2, B, 2])
        std = sb("std", [P, 2, B])
        rs_s = sb("rs_s", [P, 2, B])
        cen_t = sb("cen_t", [P, E])
        g_t = sb("g_t", [P, E])
        lb_t = sb("lb_t", [P, E])
        var_all = sb("var_all", [P, NT])
        rstd_all = sb("rstd_all", [P, NT])
        tmp_nt = sb("tmp_nt", [P, NT])
        tmp_nt2 = sb("tmp_nt2", [P, NT])
        pr = sb("pr", [P, G, J * P])
        pr_v = pr[:, :, :].rearrange("p g (j t) -> p g j t", j=J)
        xq = sb("xq", [P, 2, HALF, ROW])
        xt = sb("xt", [P, HALF, P])
        q32 = sb("q32", [P, HALF * D])
        kv32 = sb("kv32", [P, 4, HALF * D])
        k32, v32 = kv32[:, 0:2, :], kv32[:, 2:4, :]
        sq = sb("sq", [P, HALF * D])
        kvar = sb("kvar", [P, HALF * H])
        kstd = sb("kstd", [P, HALF * H])
        krs = sb("krs", [P, HALF * H])
        qs = sb("qs", [P, 2, HALF * H, 4, DK], F16)
        ks = sb("ks", [P, 2, HALF * H, 4, DK], F16)
        qqt = sb("qqt", [P, 2, J, P], F16)
        kkt = sb("kkt", [P, 2, J, P], F16)
        qt = xt
        yint = sb("yint", [P, 2, HALF, P])
        ys = sb("ys", [P, 2, J, P])
        state = sb("state", [P, B, P])
        dstate = sb("dstate", [P, HALF, P])
        res = sb("res", [P, 2, HALF, D])
        idxq = sb("idxq", [P, 2, HALF], I32)

        lnx = kv32[:, :, :].rearrange("p a n -> p (a n)").rearrange("p (a b d) -> p a b d", a=2, b=B)
        xta = ys

        wraw = sq[:, 0:3 * D]

        aff = pr[:, 0, :].rearrange("p (t e) -> p t e", e=E)
        rt1 = pr[:, 1, :].rearrange("p (t e) -> p t e", e=E)
        rt2 = pr[:, 2, :].rearrange("p (t e) -> p t e", e=E)
        rt3 = pr[:, 3, :].rearrange("p (t e) -> p t e", e=E)
        rt4 = q32[:, :].rearrange("p (t e) -> p t e", e=E)
        eidf = kv32[:, 0:2, :].rearrange("p a n -> p (a n)")[:, 0:NS * E].rearrange("p (k e) -> p k e", e=E)
        ohb = sb("ohb", [P, NT, E], BF16)
        before = sb("before", [P, P], BF16)
        onesb = sb("onesb", [P, P], BF16)
        desc = sb("desc", [P, E])
        iot_i = sb("iot_i", [P, NS], I32)
        iotk = sb("iotk", [P, NS])
        cnt = sb("cnt", [P, 5, E])
        mx = sb("mx", [P, NT])
        id_i = sb("id_i", [P, NT], I32)

        w1raw = state[:, :, :].rearrange("p (a c) d -> p a c d", a=2)
        w2raw = res[:, :, :, :].rearrange("p a b d -> p a (b d)")
        b1row = [dstate[0:1, :, :].rearrange("p a b -> p (a b)"), yint[0:1, 0, :, :].rearrange("p a b -> p (a b)")]
        w1tr = xt[:, :, :].rearrange("p a b -> p (a b)")
        lbb = yint[:, 1, 0, :]

        xs = sb("xs", [P, RING, ROW])
        xse = sb("xse", [P, 2, P])
        hb, ht = pr[:, 0:2, :], pr[:, 2:4, :]
        idxe = sb("idxe", [P, RING], I32)
        att, ye = (qs[:, a, :, :, :].rearrange("p h r d -> p (h r d)").bitcast(F32).rearrange("p (k d) -> p k d", d=D)
                   for a in range(2))
        yb = sb("yb", [P, 2, D])

        banks = [ctx.enter_context(nc.psum_tensor(f"bank{i}", [P, 512], F32)) for i in range(8)]

        S = {}

        def bcast(v, axis, n):
            shape = list(v.shape)
            return v.unsqueeze(axis).to_broadcast(shape[:axis] + [n] + shape[axis:])

        def s(name):
            if name not in S:
                S[name] = sem(name)
            return S[name]

        block = ctx.enter_context(nc.Block())

        def expert_registers(eng):
            return [eng.alloc_register(f"expert{j}") for j in range(RING + 2)]

        def load_experts(eng, regs, i):
            eng.load(regs, eid_i[0:1, bass.ds(RING * i, RING + 2)])
            return [eng.snap(r, min_val=0, max_val=E - 1) for r in regs]

        SC = [banks[0], banks[1]]
        YB, QB, KB, CB, EB, DB = banks[2], banks[3], banks[4], banks[5], banks[6], banks[7]
        qb16 = QB[:, 0:256].bitcast(F16).rearrange("p (j t) -> p j t", j=J)
        kb16 = KB[:, 0:256].bitcast(F16).rearrange("p (j t) -> p j t", j=J)

        @block.sync
        def _(sp):
            sp.dma_start(wraw, w_qkv).then_inc(s("wqkv_in"), 16)
            sp.dma_start(wo[:, :], w_o).then_inc(s("wo_in"), 16)

            def load_x(c, a):
                reach(sp, s("stats_done"), c - 1)
                sp.dma_start(resid[:, bass.ds(c * B, B), :], x_v[:, c, :, :]).then_inc(s(f"x_in{a}"), 16)

            load_x(0, 0)
            load_x(1, 1)
            with sp.Fori(1, NCH // 2, 1) as i:
                for a in range(2):
                    load_x(2 * i + a, a)

            def load_expert(e, a):
                    reach(sp, s("b1_ps"), e - 1)
                    sp.dma_start(w1raw[:, a, :, :], w1.rearrange("e (c p) d -> p e c d", p=P)[:, e, :, :])\
                      .then_inc(s(f"wraw_in{a}"), 16)
                    sp.dma_start(w2raw[:, a, :], w2.rearrange("e d f -> d e f")[:, e, :]).then_inc(s(f"wraw_in{a}"), 16)
                    sp.dma_start(b1row[a], b1.rearrange("(o e) f -> o e f", o=1)[:, e, :])\
                      .then_inc(s(f"wraw_in{a}"), 16)

            load_expert(0, 0)
            load_expert(1, 1)
            with sp.Fori(1, E // 2, 1) as i:
                for a in range(2):
                    load_expert(2 * i + a, a)

            def store_quad(n, c, half):
                sp.wait_ge(s("res_ready"), n + 1)
                sp.dma_start(attn_v[:, c, half * HALF:(half + 1) * HALF, :], res[:, half, :, :])\
                  .then_inc(s(f"attn_out{half}"), 16)

            with sp.Fori(0, NCH, 1) as c:
                for half in range(2):
                    store_quad(2 * c + half, c, half)

            for half in range(2):
                sp.wait_ge(s(f"scattered{half}"), 16 * HALF * NCH)

            def load_slots(k, a):
                reach(sp, s("ye_ready"), k - RING + 1)
                sp.dma_start(xs[:, a, :], slots_v[:, k, :]).then_inc(s(f"se_in{a}"), 16)

            for a in range(RING):
                load_slots(a, a)
            with sp.Fori(1, ROUNDS, 1) as i:
                for a in range(RING):
                    load_slots(RING * i + a, a)
            for a in range(RING):
                sp.wait_ge(s(f"out_done{a}"), 16 * ROUNDS)

        @block.gpsimd
        def _(pool):
            pool.memset(ident[:, :], 0.0).then_inc(s("pool_c"), 1)
            pool.memset(causal[:, :], 1.0).then_inc(s("pool_c"), 1)
            pool.memset(headmask[:, :], 1.0).then_inc(s("pool_c"), 1)
            pool.memset(jmask[:, :], 1.0).then_inc(s("pool_c"), 1)
            pool.memset(rt1[:, :, :], 1.0).then_inc(s("pool_c"), 1)
            pool.memset(zrow[:, :], 0.0).then_inc(s("pool_c"), 1)
            pool.wait_ge(s("pool_c"), 6)
            pool.affine_select(out=ident[:, :], in_=ident[:, :], compare_op=ALU.not_equal, fill=1.0, base=0,
                               pattern=[[-1, P]], channel_multiplier=1).then_inc(s("ident_ready"), 1)
            pool.dma_start(slots_v, bcast(zrow[:, :], 1, NS))\
                .then_inc(s("slots_zero"), 16)
            pool.dma_start(b2b[:, :, :], b2.partition_broadcast(P)).then_inc(s("b2_in"), 16)
            pool.affine_select(out=causal[:, :], in_=causal[:, :], compare_op=ALU.is_ge, fill=0.0, base=0,
                               pattern=[[1, P]], channel_multiplier=-1).then_inc(s("pool_m"), 1)
            hm = headmask[:, :].rearrange("p (g j d) -> p g j d", g=G, d=DK)
            pool.affine_select(out=hm, in_=hm, compare_op=ALU.is_ge, fill=0.0, base=0,
                               pattern=[[-DK, G], [-32, J], [0, DK]], channel_multiplier=1).then_inc(s("pool_m"), 1)
            ones_v = rt1.rearrange("p t e -> p (t e)")
            pool.affine_select(out=ones_v[:, 0:P], in_=ones_v[:, 0:P], compare_op=ALU.is_ge, fill=0.0, base=-1,
                               pattern=[[1, P]], channel_multiplier=-1).then_inc(s("pool_m"), 1)
            jm = ones_v[:, P:P + H].rearrange("p (g j) -> p g j", g=G)
            pool.affine_select(out=jm, in_=jm, compare_op=ALU.is_ge, fill=0.0, base=0,
                               pattern=[[-32, G], [-DK, J]], channel_multiplier=1).then_inc(s("pool_m"), 1)
            pool.wait_ge(s("pool_m"), 4)
            pool.affine_select(out=hm, in_=hm, compare_op=ALU.is_ge, fill=0.0, base=DK - 1,
                               pattern=[[DK, G], [32, J], [0, DK]], channel_multiplier=-1).then_inc(s("pool_m"), 1)
            pool.affine_select(out=jm, in_=jm, compare_op=ALU.is_ge, fill=0.0, base=DK - 1,
                               pattern=[[32, G], [DK, J]], channel_multiplier=-1).then_inc(s("pool_m"), 1)
            pool.iota(iot_i[:, :], [[1, NS]], base=0, channel_multiplier=0).then_inc(s("pool_m"), 1)
            pool.iota(id_i[:, :].rearrange("p (c b) -> p c b", b=B), [[-P, NCH], [-L, B]], base=NTOK,
                      channel_multiplier=-1).then_inc(s("pool_m"), 1)

            def add_resid(i, a):
                pool.wait_ge(s("lnx_ready"), 2 * i + a + 1)
                t0 = (2 * i + a) * B
                pool.tensor_tensor(resid[:, bass.ds(t0, B), :], resid[:, bass.ds(t0, B), :], lnx[:, a, :, :], ALU.add)\
                    .then_inc(s("resid_ready"), 1)

            with pool.Fori(0, NCH // 2, 1) as i:
                for a in range(2):
                    add_resid(i, a)

            def split_high(src, dst, done):
                pool.tensor_scalar(dst, src, 1.0, 0.0, ALU.mult, ALU.add).then_inc(done, 1)

            def q_high(n, par):
                reach_alone(pool, s("q_sb"), n + 1, s("pool_passed"))
                reach_alone(pool, s("qk_ps"), 4 * (n - 1), s("pool_passed"))
                split_high(q32[:, :].rearrange("p (h d) -> p h d", d=DK), qs[:, par, :, 0, :], s("q_hi"))

            def k_high(n, par):
                reach_alone(pool, s("k_sb"), n + 1, s("pool_passed"))
                split_high(k32[:, par, :].rearrange("p (h d) -> p h d", d=DK), ks[:, par, :, 0, :], s("k_hi"))

            def mask_scores(n, i, g):
                reach_alone(pool, s("sc_odd"), 8 * n + 2 * i + g // 2 + 1, s("pool_passed"))
                pool.affine_select(out=pr_v[:, g, :, :], in_=pr_v[:, g, :, :], compare_op=ALU.is_ge, fill=0.0, base=0,
                                   pattern=[[0, J], [1, P]], channel_multiplier=-1).then_inc(s("pr_odd"), 1)

            def scatter_index(n, c, half):
                if not (isinstance(c, int) and c == 0):
                    pool.wait_ge(s(f"scattered{half}"), 16 * HALF * c)
                pool.tensor_copy(idxq[:, half, :], pos_i[:, bass.ds(c * B + half * HALF, HALF)])\
                    .then_inc(s("idx_ready"), 1)
                reach_alone(pool, s("idx_ready"), n + 1, s("pool_passed"))

            def scatter_rows(i, half):
                pool.indirect_dma_start(slots_d, bass.IndirectOffsetOnAxis(ap=idxq[:, half, i:i + 1], axis=0),
                                        xq[:, half, i, :], None, bounds_check=NS * P - 1, oob_is_err=False)\
                    .then_inc(s(f"scattered{half}"), 16)

            def scatter_quad(n, c, half, i):
                if i == 0:
                    pool.wait_ge(s("xq_ready"), n + 1)
                    scatter_index(n, c, half)
                scatter_rows(i, half)

            def quad(n, c, half, more=True):
                c_next, other = (c if half == 0 else c + 1), 1 - half
                for i in range(HALF):
                    if more and i == 2:
                        q_high(n + 1, other)
                    mask_scores(n, i, 1)
                    if more and i == 0:
                        scatter_quad(n + 1, c_next, other, 0)
                    if more and i == 1:
                        scatter_quad(n + 1, c_next, other, 1)
                    if more and i == 3:
                        scatter_quad(n + 1, c_next, other, 2)
                    mask_scores(n, i, 3)
                    if more and i == 1:
                        k_high(n + 1, other)
                    if more and i == 3:
                        scatter_quad(n + 1, c_next, other, 3)
                pool.wait_ge(s("ds_sb"), n + 1)
                pool.tensor_tensor(state[:, half * HALF:(half + 1) * HALF, :], state[:, half * HALF:(half + 1) * HALF, :],
                                   dstate[:, :, :], ALU.add).then_inc(s("state_ready"), 1)

            pool.wait_ge(s("b1_ps"), E)
            pool.memset(state[:, :, :], 0.0).then_inc(s("state_zero"), 1)
            pool.wait_ge(s("state_zero"), 1)
            q_high(0, 0)
            k_high(0, 0)
            pool.wait_ge(s("slots_zero"), 16)
            for i in range(HALF):
                scatter_quad(0, 0, 0, i)
            quad(0, 0, 0)
            quad(1, 0, 1)
            with pool.Fori(1, NCH - 1, 1) as c:
                quad(2 * c, c, 0)
                quad(2 * c + 1, c, 1)
            quad(NQ - 2, NCH - 1, 0)
            quad(NQ - 1, NCH - 1, 1, more=False)

            for half in range(2):
                pool.wait_ge(s(f"attn_out{half}"), 16 * NCH)

            def gather(k, a):
                reach_alone(pool, s("se_idx"), k + 1, s("pool_passed"))
                pool.indirect_dma_start(att[:, a, :], None, attn_d,
                                        bass.IndirectOffsetOnAxis(ap=idxe[:, a:a + 1].bitcast(U32), axis=0),
                                        bounds_check=NTOK - 1, oob_is_err=False).then_inc(s(f"att_in{a}"), 16)

            def scatter_out(k, a):
                reach_alone(pool, s("ye_ready"), k + 1, s("pool_passed"))
                pool.indirect_dma_start(out_rows, bass.IndirectOffsetOnAxis(ap=idxe[:, a:a + 1].bitcast(U32), axis=0),
                                        ye[:, a, :], None, bounds_check=NTOK - 1, oob_is_err=False)\
                    .then_inc(s(f"out_done{a}"), 16)

            def round_(i, last=False):
                for a in range(RING):
                    if not last or a + AHEAD < RING:
                        gather(RING * i + a + AHEAD, (a + AHEAD) % RING)
                    scatter_out(RING * i + a, a)

            for a in range(AHEAD):
                gather(a, a)
            with pool.Fori(0, ROUNDS - 1, 1) as i:
                round_(i)
            round_(ROUNDS - 1, last=True)

        @block.scalar
        def _(act):
            act.dma_start(cen_t[:, :], centroids.rearrange("e d -> d e"), allow_slow_non_contiguous=True).then_inc(s("cen_in"), 16)
            act.dma_start(g_t[:, :], ln_g.rearrange("e d -> d e"), allow_slow_non_contiguous=True).then_inc(s("lng_in"), 16)
            act.dma_start(lb_t[:, :], ln_b.rearrange("e d -> d e"), allow_slow_non_contiguous=True).then_inc(s("lng_in"), 16)
            act.wait_ge(s("eps_ready"), 1)

            def ln_chunk(c, a):
                act.wait_ge(s("mv_ready"), c + 1)
                nc.scalar.activation(std[:, a, :], mv[:, a, :, 1], ACT.Sqrt, bias=eps[:, 0:1]).then_inc(s("std_ready"), 1)
                for hf in range(2):
                    act.wait_ge(s("xta_ps"), 2 * c + hf + 1)
                    reach(act, s("aff_ps"), 2 * c + hf - 1)
                    nc.scalar.activation(xta[:, hf, :, :], banks[hf][:, :].rearrange("p (a b) -> p a b", a=HALF),
                                         ACT.Copy).then_inc(s("xta_sb"), 1)
                act.wait_ge(s("lnx_ready"), c + 1)
                nc.scalar.activation(rows[:, bass.ds(c * B, B), 0:D], lnx[:, a, :, :], ACT.Copy)\
                    .then_inc(s("rows_ready"), 1)

            ln_chunk(0, 0)
            ln_chunk(1, 1)
            with act.Fori(1, NCH // 2, 1) as i:
                for a in range(2):
                    ln_chunk(2 * i + a, a)

            act.wait_ge(s("var2_ready"), 1)
            nc.scalar.activation(tmp_nt2[:, :], tmp_nt[:, :], ACT.Sqrt, bias=eps[:, 0:1]).then_inc(s("std2_ready"), 1)

            def prep(e, a):
                act.wait_ge(s("lng_in"), 32)
                act.wait_ge(s("w1t_ps"), e + 1)
                reach(act, s("b1_ps"), e)
                nc.scalar.activation(w1tr, banks[2][:, :], ACT.Copy)
                nc.scalar.activation(lbb, ones[:, :], ACT.Copy, scale=lb_t[:, bass.ds(e, 1)]).then_inc(s("w1tr_ready"), 1)
                nc.scalar.activation(w1t[:, e, :], banks[2][:, :], ACT.Copy, scale=g_t[:, bass.ds(e, 1)])\
                    .then_inc(s("w1t_ready"), 1)
                act.wait_ge(s("w2t_ps"), e + 1)
                nc.scalar.activation(w2t[:, e, :, :], banks[3][:, :].rearrange("p (c d) -> p c d", c=FC), ACT.Copy)\
                    .then_inc(s("w2t_ready"), 1)
                act.wait_ge(s("b1_ps"), e + 1)
                nc.scalar.activation(b1b[:, e, :], banks[4][:, :], ACT.Copy).then_inc(s("b1b_ready"), 1)

            prep(0, 0)
            prep(1, 1)
            with act.Fori(1, E // 2, 1) as i:
                prep(2 * i, 0)
                prep(2 * i + 1, 1)

            act.wait_ge(s("mx_ready"), 1)
            nc.scalar.activation(rows[:, :, D + 1], mx[:, :], ACT.Sigmoid).then_inc(s("gate_ready"), 1)

            act.wait_ge(s("qbound"), 1)
            nc.scalar.activation(tmp_nt[:, 0:H], tmp_nt2[:, 0:H], ACT.Sqrt, scale=float(P) / (QTOP * QTOP))\
                .then_inc(s("qbound_root"), 1)

            def x_transposed(n):
                act.wait_ge(s("xt_ps"), n + 1)
                reach(act, s("in_ps"), n)
                nc.scalar.activation(xt[:, :, :].rearrange("p a b -> p (a b)"), EB[:, :], ACT.Copy).then_inc(s("xt_sb"), 1)

            def q_copy(n):
                act.wait_ge(s("q_ps"), n + 1)
                reach(act, s("q_lo"), n)
                reach(act, s("qt_ps"), n)
                nc.scalar.activation(q32[:, :], CB[:, :], ACT.Copy).then_inc(s("q_sb"), 1)

            def k_square(n):
                act.wait_ge(s("k_ps"), n + 1)
                reach(act, s("kvar_ready"), n)
                nc.scalar.activation(sq[:, :], EB[:, :], ACT.Square).then_inc(s("sq_ready"), 1)

            def k_root(n):
                act.wait_ge(s("kvar_ready"), n + 1)
                reach(act, s("k_sb"), n)
                nc.scalar.activation(kstd[:, :], kvar[:, :], ACT.Sqrt, scale=1.0 / DK, bias=eps[:, 0:1])\
                    .then_inc(s("kstd_ready"), 1)

            def v_copy(n, par):
                act.wait_ge(s("v_ps"), n + 1)
                reach(act, s("ds_ps"), n - 1)
                nc.scalar.activation(v32[:, par, :], CB[:, :], ACT.Copy).then_inc(s("v_sb"), 1)

            def q_transposed(n):
                act.wait_ge(s("qt_ps"), n + 1)
                act.wait_ge(s("v_ps"), n + 1)
                nc.scalar.activation(qt[:, :, :].rearrange("p a b -> p (a b)"), EB[:, :], ACT.Copy).then_inc(s("qt_sb"), 1)

            def qq_copy(m, a):
                act.wait_ge(s("qk_ps"), m + 1)
                reach(act, s("sc_ps"), 4 * (m - 1))
                nc.scalar.activation(qqt[:, a, :, :], qb16, ACT.Copy).then_inc(s("qq_sb"), 1)

            def score_copy(m, g):
                act.wait_ge(s("sc_ps"), 4 * m + g + 1)
                reach(act, s("av_ps"), 4 * (m - 1) + g + 1)
                nc.scalar.activation(pr[:, g, :], SC[1][:, :], ACT.Copy).then_inc(s("sc_odd"), 1)

            def y_copy(m, a):
                act.wait_ge(s("av_ps"), 4 * m + 4)
                reach(act, s("out_ps"), m - 1)
                nc.scalar.activation(ys[:, a, :, :].rearrange("p j t -> p (j t)"), YB[:, :], ACT.Copy).then_inc(s("y_sb"), 1)

            def quad(n, c, half, first=False, more=True):
                for i in range(HALF):
                    m = 4 * n + i
                    score_copy(m, 1)
                    if not (first and i == 0):
                        y_copy(m - 1, (i + 1) % 2)
                    if more and i == 0:
                        x_transposed(n + 1)
                    if more and i == 1:
                        k_root(n + 1)
                    if more or i < 3:
                        qq_copy(m + 1, (i + 1) % 2)
                    if more and i == 1:
                        q_copy(n + 1)
                    if more and i == 2:
                        v_copy(n + 1, 1 - half)
                    score_copy(m, 3)
                    if more and i == 0:
                        k_square(n + 1)
                    if more and i == 2:
                        q_transposed(n + 1)

            act.wait_ge(s("b1b_ready"), E)
            x_transposed(0)
            q_copy(0)
            k_square(0)
            k_root(0)
            v_copy(0, 0)
            q_transposed(0)
            qq_copy(0, 0)
            quad(0, 0, 0, first=True)
            quad(1, 0, 1)
            with act.Fori(1, NCH - 1, 1) as c:
                quad(2 * c, c, 0)
                quad(2 * c + 1, c, 1)
            quad(NQ - 2, NCH - 1, 0)
            quad(NQ - 1, NCH - 1, 1, more=False)
            y_copy(NT - 1, 1)

            def se_x(k, a):
                act.wait_ge(s("sex_ps"), k + 1)
                reach(act, s("h_ps"), k - 1)
                nc.scalar.activation(xse[:, a % 2, :], banks[6 + a % 2][:, 0:P], ACT.Copy).then_inc(s("sex_sb"), 1)

            def se_relu(k, a):
                act.wait_ge(s("ht_ps"), k + 1)
                reach(act, s("ye_ps"), k - 1)
                nc.scalar.activation(ht[:, a % 2, :], banks[2 + a % 2][:, :], ACT.Relu).then_inc(s("ht_sb"), 1)

            se_x(0, 0)
            se_x(1, 1)
            se_x(2, 0)
            for k in range(2):
                se_x(k + 3, 1 - k)
                se_relu(k, k)
            with act.Fori(1, NS // 2 - 2, 1) as i:
                for a in range(2):
                    se_x(2 * i + a + 3, 1 - a)
                    se_relu(2 * i + a, a)
            se_x(NS - 1, 1)
            for k in range(NS - 4, NS):
                se_relu(k, k % 2)

        @block.vector
        def _(dve):
            chain = [0]

            def link(ins):
                chain[0] += 1
                ins.then_inc(s("dve_chain"), 1)
                dve.wait_ge(s("dve_chain"), chain[0])

            nc.vector.memset(eps[:, :], EPS).then_inc(s("eps_ready"), 1)
            nc.vector.memset(ones[:, :], 1.0).then_inc(s("ones_ready"), 1)
            nc.vector.memset(onesb[:, :], 1.0)
            nc.vector.memset(eid_i[:, 0:1], 0)
            nc.vector.memset(eid_i[:, NS + 1:NS + RING], 0)
            for e in range(E):
                nc.vector.memset(desc[:, e:e + 1], float(E - e))

            def ln_chunk(i, a):
                c = 2 * i + a
                dve.wait_ge(s(f"x_in{a}"), 16 * (i + 1))
                for b in range(B):
                    last = nc.vector.bn_stats(stats[:, a, b, :], resid[:, c * B + b, :])
                last.then_inc(s("stats_done"), 1)
                reach_alone(dve, s("stats_done"), c + 1, s("dve_passed"))
                for b in range(B):
                    last = nc.vector.bn_aggr(mv[:, a, b, :], stats[:, a, b, :])
                last.then_inc(s("mv_ready"), 1)
                dve.wait_ge(s("mv_ready"), c + 1)
                nc.vector.tensor_copy(var_all[:, bass.ds(c * B, B)], mv[:, a, :, 1])
                dve.wait_ge(s("std_ready"), c + 1)
                nc.vector.reciprocal(rs_s[:, a, :], std[:, a, :]).then_inc(s("rs_done"), 1)
                dve.wait_ge(s("rs_done"), c + 1)
                nc.vector.tensor_copy(rstd_all[:, bass.ds(c * B, B)], rs_s[:, a, :])
                reach(dve, s("xta_ps"), 2 * (c - 1))
                reach(dve, s("resid_ready"), c - 1)
                reach(dve, s("rows_ready"), c - 1)
                for b in range(B):
                    last = nc.vector.tensor_scalar(lnx[:, a, b, :], resid[:, c * B + b, :], mv[:, a, b, 0:1],
                                                   rs_s[:, a, b:b + 1], ALU.subtract, ALU.mult)
                last.then_inc(s("lnx_ready"), 1)

            ln_chunk(0, 0)
            ln_chunk(0, 1)
            with dve.Fori(1, NCH // 2, 1) as i:
                for a in range(2):
                    ln_chunk(i, a)

            dve.wait_ge(s("lnx_ready"), NCH)
            link(nc.vector.tensor_tensor(tmp_nt[:, :], rstd_all[:, :], rstd_all[:, :], ALU.mult))
            nc.vector.tensor_tensor(tmp_nt[:, :], tmp_nt[:, :], var_all[:, :], ALU.mult).then_inc(s("var2_ready"), 1)

            dve.wait_ge(s("aff_ps"), 2 * NCH)
            dve.wait_ge(s("pool_m"), 8)
            nc.vector.tensor_copy(before[:, :], rt1.rearrange("p t e -> p (t e)")[:, 0:P])
            link(nc.vector.tensor_copy(jmask[:, :], rt1.rearrange("p t e -> p (t e)")[:, P:P + J]))
            for g in range(1, G):
                link(nc.vector.tensor_tensor(jmask[:, :], jmask[:, :],
                                             rt1.rearrange("p t e -> p (t e)")[:, P + J * g:P + J * (g + 1)], ALU.add))
            nc.vector.tensor_copy(iotk[:, :], iot_i[:, :])
            link(nc.vector.tensor_copy(aff, banks[7][:, :].rearrange("p (t e) -> p t e", e=E)))

            def over_e(v):
                return bcast(v, 2, E)

            def over_t(v, n=NT):
                return bcast(v, 1, n)

            nc.vector.tensor_reduce(out=mx[:, :], in_=aff, axis=AX, op=ALU.max).then_inc(s("mx_ready"), 1)
            dve.wait_ge(s("mx_ready"), 1)
            link(nc.vector.tensor_tensor(rt2, aff, over_e(mx[:, :]), ALU.is_ge))
            link(nc.vector.tensor_tensor(rt2, rt2, over_t(desc[:, :]), ALU.mult))
            link(nc.vector.tensor_reduce(out=rstd_all[:, :], in_=rt2, axis=AX, op=ALU.max))
            nc.vector.tensor_tensor(ohb[:, :, :], rt2, over_e(rstd_all[:, :]), ALU.is_equal).then_inc(s("oh_ready"), 1)
            dve.wait_ge(s("std2_ready"), 1)
            link(nc.vector.reciprocal(rows[:, :, D], tmp_nt2[:, :]))
            nc.vector.tensor_copy(rows[:, :, D + 2], id_i[:, :])
            nc.vector.memset(rows[:, :, D + 3], 0.0)
            dve.wait_ge(s("rank_ps"), 2)
            link(nc.vector.tensor_copy(rt3, banks[6][:, :].rearrange("p (t e) -> p t e", e=E)))
            nc.vector.tensor_copy(rt1, rt3)
            cur, nxt = rt3, rt4
            step = 1
            while step < NT:
                nc.vector.tensor_copy(nxt[:, 0:step, :], cur[:, 0:step, :])
                link(nc.vector.tensor_tensor(nxt[:, step:NT, :], cur[:, step:NT, :], cur[:, 0:NT - step, :], ALU.add))
                cur, nxt = nxt, cur
                step *= 2
            tiles_cmp = aff.rearrange("p t e -> p (t e)").rearrange("p (e k) -> p e k", e=E)
            link(nc.vector.tensor_scalar(cnt[:, 0, :], cur[:, NT - 1, :], 1.0 / P, None, ALU.mult))
            link(nc.vector.tensor_tensor(tiles_cmp, bcast(cnt[:, 0, :], 2, NT),
                                         over_t(iotk[:, 0:NT], E), ALU.is_gt))
            link(nc.vector.tensor_reduce(out=cnt[:, 1, :], in_=tiles_cmp, axis=AX, op=ALU.add))
            link(nc.vector.tensor_copy(cnt[:, 2, :], cnt[:, 1, :]))
            a_, b_ = 2, 3
            step = 1
            while step < E:
                nc.vector.tensor_copy(cnt[:, b_, 0:step], cnt[:, a_, 0:step])
                link(nc.vector.tensor_tensor(cnt[:, b_, step:E], cnt[:, a_, step:E], cnt[:, a_, 0:E - step], ALU.add))
                a_, b_ = b_, a_
                step *= 2
            dve.wait_ge(s("rows_ready"), NCH)
            dve.wait_ge(s("resid_ready"), NCH)
            link(nc.vector.tensor_tensor(eidf, over_t(cnt[:, a_, :], NS),
                                         bcast(iotk[:, :], 2, E), ALU.is_le))
            link(nc.vector.tensor_reduce(out=iotk[:, :], in_=eidf, axis=AX, op=ALU.add))
            nc.vector.tensor_scalar(eid_i[:, 1:NS + 1], iotk[:, :], float(E - 1), None, ALU.min).then_inc(s("eid_ready"), 1)
            link(nc.vector.tensor_tensor(cnt[:, 4, :], cnt[:, a_, :], cnt[:, 1, :], ALU.subtract))
            link(nc.vector.tensor_scalar(cnt[:, 4, :], cnt[:, 4, :], float(P), None, ALU.mult))
            link(nc.vector.tensor_tensor(cur, cur, rt1, ALU.subtract))
            link(nc.vector.tensor_tensor(cur, cur, over_t(cnt[:, 4, :]), ALU.add))
            link(nc.vector.tensor_tensor(cur, banks[5][:, :].rearrange("p (t e) -> p t e", e=E), cur, ALU.add))
            link(nc.vector.tensor_tensor(cur, cur, ohb[:, :, :], ALU.mult))
            link(nc.vector.tensor_reduce(out=tmp_nt[:, :], in_=cur, axis=AX, op=ALU.add))
            nc.vector.tensor_copy(pos_i[:, :], tmp_nt[:, :]).then_inc(s("route_done"), 1)

            dve.wait_ge(s("wqkv_in"), 16)
            for part in range(2):
                nc.vector.tensor_copy(wqkv[:, part * D:(part + 1) * D].rearrange("p (j g d) -> p j g d", j=J, g=G),
                                      wraw[:, part * D:(part + 1) * D].rearrange("p (g j d) -> p j g d", j=J, g=G))
            link(nc.vector.tensor_copy(wqkv[:, 2 * D:3 * D], wraw[:, 2 * D:3 * D]))
            wk = wqkv[:, D:2 * D].rearrange("p (h d) -> p h d", d=DK)
            link(nc.vector.tensor_reduce(out=tmp_nt[:, 0:H], in_=wk, axis=AX, op=ALU.add))
            link(nc.vector.tensor_scalar(tmp_nt[:, 0:H], tmp_nt[:, 0:H], 1.0 / DK, None, ALU.mult))
            nc.vector.tensor_tensor(wk, wk, bcast(tmp_nt[:, 0:H], 2, DK),
                                    ALU.subtract)
            nc.vector.tensor_tensor(sq[:, 0:D], wqkv[:, 0:D], wqkv[:, 0:D], ALU.mult).then_inc(s("wq_sq"), 1)
            dve.wait_ge(s("norm_ps"), 1)
            nc.vector.tensor_reduce(out=tmp_nt2[:, 0:H], in_=banks[6][:, 0:D].rearrange("p (h d) -> p h d", d=DK),
                                    axis=AX, op=ALU.max).then_inc(s("qbound"), 1)
            dve.wait_ge(s("qbound_root"), 1)
            link(nc.vector.tensor_scalar(tmp_nt[:, 0:H], tmp_nt[:, 0:H], TINY, None, ALU.max))
            link(nc.vector.reciprocal(tmp_nt[:, H:2 * H], tmp_nt[:, 0:H]))
            wq = wqkv[:, 0:D].rearrange("p (h d) -> p h d", d=DK)
            nc.vector.tensor_tensor(wq, wq, bcast(tmp_nt[:, H:2 * H], 2, DK),
                                    ALU.mult).then_inc(s("wqkv_ready"), 1)
            dve.wait_ge(s("ident_ready"), 1)
            dve.wait_ge(s("wo_in"), 16)
            bound = tmp_nt[:, 0:H]
            per = sq[:, D:2 * D].rearrange("p (h d) -> p h d", d=DK)
            idv = ident[:, :].rearrange("p (h d) -> p h d", d=DK)
            for g in range(G):
                last = nc.vector.tensor_tensor(per[:, J * g:J * (g + 1), :], idv[:, J * g:J * (g + 1), :],
                                               bcast(bound[:, g:H:G], 2, DK), ALU.mult)
            link(last)
            link(nc.vector.tensor_reduce(out=cnt[:, 0, 0:1], in_=sq[:, D:2 * D], axis=AX, op=ALU.add))
            link(nc.vector.tensor_scalar(wo[:, :], wo[:, :], cnt[:, 0, 0:1], None, ALU.mult))
            for j in range(J):
                last = nc.vector.tensor_scalar(wom[:, j, :], wo[:, :], jmask[:, j:j + 1], None, ALU.mult)
            nc.vector.tensor_copy(identh[:, :], ident[:, :]).then_inc(s("wo_ready"), 1)

            def x_copy(n, c, half):
                reach(dve, s("xt_ps"), n - 1)
                if not (isinstance(c, int) and c == 0):
                    dve.wait_ge(s(f"scattered{half}"), 16 * HALF * c)
                nc.vector.tensor_copy(xq[:, half, :, :], rows[:, bass.ds(c * B + half * HALF, HALF), :])\
                    .then_inc(s("xq_ready"), 1)

            def k_var(n):
                dve.wait_ge(s("sq_ready"), n + 1)
                nc.vector.tensor_reduce(out=kvar[:, :], in_=sq[:, :].rearrange("p (h d) -> p h d", d=DK), axis=AX,
                                        op=ALU.add).then_inc(s("kvar_ready"), 1)

            def k_norm(n, par):
                dve.wait_ge(s("kstd_ready"), n + 1)
                nc.vector.reciprocal(krs[:, :], kstd[:, :]).then_inc(s("krs_ready"), 1)
                dve.wait_ge(s("krs_ready"), n + 1)
                reach(dve, s("ds_ps"), n - 1)
                nc.vector.tensor_tensor(k32[:, par, :].rearrange("p (h d) -> p h d", d=DK),
                                        EB[:, :].rearrange("p (h d) -> p h d", d=DK),
                                        bcast(krs[:, :], 2, DK), ALU.mult)\
                    .then_inc(s("k_sb"), 1)

            def q_low(n, par):
                dve.wait_ge(s("q_hi"), n + 1)
                nc.vector.tensor_tensor(qs[:, par, :, 2, :], q32[:, :].rearrange("p (h d) -> p h d", d=DK),
                                        qs[:, par, :, 0, :], ALU.subtract).then_inc(s("q_lo"), 1)
                dve.wait_ge(s("q_lo"), n + 1)
                nc.vector.tensor_copy(qs[:, par, :, 1::2, :], qs[:, par, :, 0::2, :]).then_inc(s("q_parts"), 1)

            def k_low(n, par):
                dve.wait_ge(s("k_hi"), n + 1)
                nc.vector.tensor_tensor(ks[:, par, :, 1, :], k32[:, par, :].rearrange("p (h d) -> p h d", d=DK),
                                        ks[:, par, :, 0, :], ALU.subtract).then_inc(s("k_lo"), 1)
                dve.wait_ge(s("k_lo"), n + 1)
                nc.vector.tensor_copy(ks[:, par, :, 2:4, :], ks[:, par, :, 0:2, :]).then_inc(s("k_parts"), 1)

            def kk_copy(m, a):
                dve.wait_ge(s("qk_ps"), m + 1)
                reach(dve, s("sc_ps"), 4 * (m - 1))
                nc.vector.tensor_copy(kkt[:, a, :, :], kb16).then_inc(s("kk_sb"), 1)

            def score_mask(m, g):
                dve.wait_ge(s("sc_ps"), 4 * m + g + 1)
                reach(dve, s("av_ps"), 4 * (m - 1) + g + 1)
                nc.vector.tensor_tensor(pr_v[:, g, :, :], SC[0][:, :].rearrange("p (j t) -> p j t", j=J),
                                        bcast(causal[:, :], 1, J), ALU.mult)\
                    .then_inc(s("pr_even"), 1)

            def inter_copy(n, half):
                dve.wait_ge(s("in_ps"), n + 1)
                reach(dve, s("out_ps"), 4 * (n - 1))
                nc.vector.tensor_copy(yint[:, half, :, :].rearrange("p a b -> p (a b)"), EB[:, :]).then_inc(s("yi_sb"), 1)

            def dstate_mask(n):
                dve.wait_ge(s("ds_ps"), n + 1)
                reach(dve, s("state_ready"), n)
                nc.vector.tensor_tensor(dstate[:, :, :], CB[:, :].rearrange("p (a b) -> p a b", a=HALF),
                                        bcast(headmask[:, :], 1, HALF), ALU.mult)\
                    .then_inc(s("ds_sb"), 1)

            def result(n, c, half):
                dve.wait_ge(s("out_ps"), 4 * n + 4)
                if not (isinstance(c, int) and c == 0):
                    dve.wait_ge(s(f"attn_out{half}"), 16 * c)
                nc.vector.tensor_tensor(res[:, half, :, :], DB[:, :].rearrange("p (a b) -> p a b", a=HALF),
                                        resid[:, bass.ds(c * B + half * HALF, HALF), :], ALU.add)\
                    .then_inc(s("res_ready"), 1)

            def quad(n, c, half, first=False, more=True, ahead=True):
                other = 1 - half
                for i in range(HALF):
                    m = 4 * n + i
                    score_mask(m, 0)
                    if more or i < 3:
                        kk_copy(m + 1, (i + 1) % 2)
                    if more and i == 1:
                        k_var(n + 1)
                    if more and i == 2:
                        k_low(n + 1, other)
                    if more and i == 3:
                        dstate_mask(n)
                    score_mask(m, 2)
                    if more and i == 1:
                        k_norm(n + 1, other)
                    if not first and i == 0:
                        result(n - 1, c if half == 1 else c - 1, other)
                    if more and i == 2:
                        q_low(n + 1, other)
                    if more and i == 3:
                        inter_copy(n + 1, other)
                    if ahead and i == 3:
                        x_copy(n + 2, c + 1, half)
                if not more:
                    dstate_mask(n)

            dve.wait_ge(s("gate_ready"), 1)
            dve.wait_ge(s("rows_ready"), NCH)
            dve.wait_ge(s("resid_ready"), NCH)
            x_copy(0, 0, 0)
            x_copy(1, 0, 1)
            k_var(0)
            k_norm(0, 0)
            q_low(0, 0)
            k_low(0, 0)
            kk_copy(0, 0)
            inter_copy(0, 0)
            quad(0, 0, 0, first=True)
            quad(1, 0, 1)
            with dve.Fori(1, NCH - 1, 1) as c:
                quad(2 * c, c, 0)
                quad(2 * c + 1, c, 1)
            quad(NQ - 2, NCH - 1, 0, ahead=False)
            quad(NQ - 1, NCH - 1, 1, more=False, ahead=False)
            result(NQ - 1, NCH - 1, 1)

            dve.wait_ge(s("eid_ready"), 1)
            dve.wait_ge(s("b2_in"), 16)
            dve.wait_ge(s("b1b_ready"), E)
            dve.wait_ge(s("qk_ps"), NT)
            nc.vector.memset(att, 0.0).then_inc(s("att_zero"), 1)
            dve.wait_ge(s("att_zero"), 1)

            def se_index(k, a, rnd):
                dve.wait_ge(s(f"se_in{a}"), 16 * (rnd + 1))
                reach(dve, s(f"out_done{a}"), 16 * rnd)
                nc.vector.tensor_scalar(idxe[:, a:a + 1], xs[:, a, D + 2:D + 3], -1.0, float(NTOK), ALU.mult, ALU.add)\
                    .then_inc(s("se_idx"), 1)

            def se_bias(k, a, e):
                dve.wait_ge(s("h_ps"), k + 1)
                reach(dve, s("ht_ps"), k - 1)
                nc.vector.scalar_tensor_tensor(out=hb[:, a % 2, :], in0=banks[a % 2][:, :], scalar=xs[:, a, D:D + 1],
                                               in1=b1b[:, e, :], op0=ALU.mult, op1=ALU.add).then_inc(s("hb_ready"), 1)

            def se_result(k, a, rnd, e):
                dve.wait_ge(s("ye_ps"), k + 1)
                nc.vector.tensor_tensor(yb[:, a % 2, :], banks[4 + a % 2][:, 0:D], b2b[:, e, :], ALU.add)\
                    .then_inc(s("yb_done"), 1)
                dve.wait_ge(s(f"att_in{a}"), 16 * (rnd + 1))
                dve.wait_ge(s("yb_done"), k + 1)
                nc.vector.scalar_tensor_tensor(out=ye[:, a, :], in0=yb[:, a % 2, :], scalar=xs[:, a, D + 1:D + 2],
                                               in1=att[:, a, :], op0=ALU.mult, op1=ALU.add).then_inc(s("ye_ready"), 1)

            def expert_round(i, e, first=False, last=False):
                for a in range(RING):
                    k = RING * i + a
                    if not last or a < RING - 1:
                        se_bias(k + 1, (a + 1) % RING, e[a + 2])
                    if a > 0:
                        se_result(k - 1, a - 1, i, e[a])
                    elif not first:
                        se_result(k - 1, RING - 1, i - 1, e[a])
                    if not last or a + AHEAD < RING:
                        se_index(k + AHEAD, (a + AHEAD) % RING, i + (a + AHEAD) // RING)

            for a in range(AHEAD):
                se_index(a, a, 0)
            regs = expert_registers(dve)
            e = load_experts(dve, regs, 0)
            se_bias(0, 0, e[1])
            expert_round(0, e, first=True)
            with dve.Fori(1, ROUNDS - 1, 1) as i:
                expert_round(i, load_experts(dve, regs, i))
            e = load_experts(dve, regs, ROUNDS - 1)
            expert_round(ROUNDS - 1, e, last=True)
            se_result(NS - 1, RING - 1, ROUNDS - 1, e[RING])

        @block.tensor
        def _(pe):
            mm = nc.tensor.matmul
            pe.wait_ge(s("ident_ready"), 1)
            pe.wait_ge(s("cen_in"), 16)

            def ln_chunk(c, a):
                pe.wait_ge(s("lnx_ready"), c + 1)
                for hf in range(2):
                    reach(pe, s("xta_sb"), 2 * (c - 1) + hf + 1)
                    for b in range(HALF):
                        last = nc.tensor.transpose(banks[hf][:, b * P:(b + 1) * P], lnx[:, a, hf * HALF + b, :], ident[:, :])
                    last.then_inc(s("xta_ps"), 1)
                for hf in range(2):
                    pe.wait_ge(s("xta_sb"), 2 * c + hf + 1)
                    for b in range(HALF):
                        last = mm(banks[7][:, bass.ds((c * B + hf * HALF + b) * E, E)], xta[:, hf, b, :], cen_t[:, :],
                                  start=True, stop=True)
                    last.then_inc(s("aff_ps"), 1)

            ln_chunk(0, 0)
            ln_chunk(1, 1)
            with pe.Fori(1, NCH // 2, 1) as i:
                for a in range(2):
                    ln_chunk(2 * i + a, a)

            pe.wait_ge(s("ones_ready"), 1)

            def prep(e, a, i):
                pe.wait_ge(s(f"wraw_in{a}"), 48 * (i + 1))
                reach(pe, s("w1t_ready"), e)
                for c in range(FC):
                    last = nc.tensor.transpose(banks[2][:, c * P:(c + 1) * P], w1raw[:, a, c, :], ident[:, :])
                last.then_inc(s("w1t_ps"), 1)
                reach(pe, s("w2t_ready"), e)
                for c in range(FC):
                    last = nc.tensor.transpose(banks[3][:, c * P:(c + 1) * P], w2raw[:, a, c * P:(c + 1) * P], ident[:, :])
                last.then_inc(s("w2t_ps"), 1)
                pe.wait_ge(s("w1tr_ready"), e + 1)
                reach(pe, s("b1b_ready"), e)
                mm(banks[4][:, :], lbb, w1tr, start=True, stop=False)
                mm(banks[4][:, :], ones[0:1, :], b1row[a], start=False, stop=True).then_inc(s("b1_ps"), 1)

            prep(0, 0, 0)
            prep(1, 1, 0)
            with pe.Fori(1, E // 2, 1) as i:
                for a in range(2):
                    prep(2 * i + a, a, i)

            pe.wait_ge(s("oh_ready"), 1)
            ohv = ohb[:, :, :].rearrange("p t e -> p (t e)")
            mm(banks[5][:, :], before[:, :], ohv, start=True, stop=True).then_inc(s("rank_ps"), 1)
            mm(banks[6][:, :], onesb[:, :], ohv, start=True, stop=True).then_inc(s("rank_ps"), 1)

            pe.wait_ge(s("wq_sq"), 1)
            mm(banks[6][:, 0:D], ones[:, :], sq[:, 0:D], start=True, stop=True).then_inc(s("norm_ps"), 1)

            def x_trans(n, par):
                pe.wait_ge(s("xq_ready"), n + 1)
                reach(pe, s("yi_sb"), n)
                for i in range(HALF):
                    last = nc.tensor.transpose(EB[:, i * P:(i + 1) * P], xq[:, par, i, 0:D], ident[:, :])
                last.then_inc(s("xt_ps"), 1)

            def project(bank, col, done):
                for i in range(HALF):
                    last = mm(bank[:, i * P:(i + 1) * P], xt[:, i, :], wqkv[:, col:col + D], start=True, stop=True)
                last.then_inc(s(done), 1)

            def q_project(n):
                reach(pe, s("ds_sb"), n - 1)
                project(CB, 0, "q_ps")

            def k_project(n):
                pe.wait_ge(s("xt_sb"), n + 1)
                project(EB, D, "k_ps")

            def v_project(n):
                pe.wait_ge(s("q_sb"), n + 1)
                project(CB, 2 * D, "v_ps")

            def q_trans(n):
                pe.wait_ge(s("k_sb"), n + 1)
                for i in range(HALF):
                    last = nc.tensor.transpose(EB[:, i * P:(i + 1) * P], q32[:, i * D:(i + 1) * D], ident[:, :])
                last.then_inc(s("qt_ps"), 1)

            def qk_trans(m, n, i, par):
                if i == 0:
                    pe.wait_ge(s("q_parts"), n + 1)
                    pe.wait_ge(s("k_parts"), n + 1)
                reach(pe, s("qq_sb"), m)
                reach(pe, s("kk_sb"), m)
                for j in range(J):
                    h0 = i * H + j * G
                    qv = qs[:, par, h0:h0 + G, :, :].rearrange("p g r d -> p (g r d)")
                    nc.tensor.transpose(qb16[:, j, :], qv, identh[:, :])
                    kv = ks[:, par, h0:h0 + G, :, :].rearrange("p g r d -> p (g r d)")
                    last = nc.tensor.transpose(kb16[:, j, :], kv, identh[:, :])
                last.then_inc(s("qk_ps"), 1)

            def scores(m, i, g):
                if g == 0:
                    pe.wait_ge(s("qq_sb"), m + 1)
                    pe.wait_ge(s("kk_sb"), m + 1)
                reach(pe, s("sc_odd" if g % 2 else "pr_even"), 2 * m + g // 2)
                for j in range(J):
                    last = mm(SC[g % 2][:, j * P:(j + 1) * P], kkt[32 * g:32 * (g + 1), i % 2, j, :],
                              qqt[32 * g:32 * (g + 1), i % 2, j, :], start=True, stop=True)
                last.then_inc(s("sc_ps"), 1)

            def weighted(m, i, par, g):
                if g == 0:
                    reach(pe, s("y_sb"), m)
                pe.wait_ge(s("pr_odd" if g % 2 else "pr_even"), 2 * m + g // 2 + 1)
                mm(YB[32 * g:32 * (g + 1), :], v32[:, par, i * D + 32 * g:i * D + 32 * (g + 1)], pr[:, g, :], start=True, stop=True).then_inc(s("av_ps"), 1)

            def output(m, n, i, half):
                if i == 0:
                    reach(pe, s("res_ready"), n)
                    pe.wait_ge(s("yi_sb"), n + 1)
                pe.wait_ge(s("y_sb"), m + 1)
                o = DB[:, i * D:(i + 1) * D]
                mm(o, yint[:, half, i, :], wo[:, :], start=True, stop=False)
                for j in range(J):
                    last = mm(o, ys[:, i % 2, j, :], wom[:, j, :], start=False, stop=(j == J - 1))
                last.then_inc(s("out_ps"), 1)

            def inter(n, half):
                pe.wait_ge(s("qt_sb"), n + 1)
                reach(pe, s("state_ready"), n - 1)
                for i in range(HALF):
                    last = mm(EB[:, i * P:(i + 1) * P], state[:, half * HALF + i, :], qt[:, i, :], start=True, stop=True)
                last.then_inc(s("in_ps"), 1)

            def state_step(n, par, more):
                pe.wait_ge(s("v_sb"), n + 2 if more else n + 1)
                for i in range(HALF):
                    last = mm(CB[:, i * P:(i + 1) * P], k32[:, par, i * D:(i + 1) * D], v32[:, par, i * D:(i + 1) * D],
                              start=True, stop=True)
                last.then_inc(s("ds_ps"), 1)

            def quad(n, c, half, first=False, more=True):
                other = 1 - half
                for i in range(HALF):
                    m = 4 * n + i
                    before = not (first and i == 0)
                    i_b, par_b = (i - 1) % HALF, half if i else other
                    scores(m, i, 0)
                    if before:
                        weighted(m - 1, i_b, par_b, 2)
                    if i < 3:
                        qk_trans(m + 1, n, i + 1, half)
                    if more and i == 0:
                        x_trans(n + 1, other)
                    if more and i == 3:
                        state_step(n, half, more)
                    scores(m, i, 1)
                    if before:
                        weighted(m - 1, i_b, par_b, 3)
                    if more and i == 1:
                        q_project(n + 1)
                    if more and i == 2:
                        v_project(n + 1)
                    if more and i == 3:
                        qk_trans(m + 1, n + 1, 0, other)
                    scores(m, i, 2)
                    weighted(m, i, half, 0)
                    if more and i == 0:
                        k_project(n + 1)
                    if more and i == 2:
                        q_trans(n + 1)
                    if more and i == 3:
                        inter(n + 1, other)
                    scores(m, i, 3)
                    weighted(m, i, half, 1)
                    if before:
                        output(m - 1, n if i else n - 1, i_b, par_b)
                if not more:
                    state_step(n, half, more)

            pe.wait_ge(s("wqkv_ready"), 1)
            pe.wait_ge(s("wo_ready"), 1)
            pe.wait_ge(s("route_done"), 1)
            pe.wait_ge(s("b1b_ready"), E)
            pe.wait_ge(s("state_zero"), 1)
            x_trans(0, 0)
            k_project(0)
            q_project(0)
            v_project(0)
            q_trans(0)
            qk_trans(0, 0, 0, 0)
            inter(0, 0)
            quad(0, 0, 0, first=True)
            quad(1, 0, 1)
            with pe.Fori(1, NCH - 1, 1) as c:
                quad(2 * c, c, 0)
                quad(2 * c + 1, c, 1)
            quad(NQ - 2, NCH - 1, 0)
            quad(NQ - 1, NCH - 1, 1, more=False)
            weighted(NT - 1, HALF - 1, 1, 2)
            weighted(NT - 1, HALF - 1, 1, 3)
            output(NT - 1, NQ - 1, HALF - 1, 1)

            pe.wait_ge(s("res_ready"), NQ)
            pe.wait_ge(s("ds_sb"), NQ)
            pe.wait_ge(s("w1t_ready"), E)
            pe.wait_ge(s("w2t_ready"), E)
            pe.wait_ge(s("eid_ready"), 1)

            def se_trans(k, a, rnd):
                pe.wait_ge(s(f"se_in{a}"), 16 * (rnd + 1))
                reach(pe, s("sex_sb"), k - 1)
                nc.tensor.transpose(banks[6 + a % 2][:, 0:P], xs[:, a, 0:D], ident[:, :]).then_inc(s("sex_ps"), 1)

            def se_up(k, a, e):
                pe.wait_ge(s("sex_sb"), k + 1)
                reach(pe, s("hb_ready"), k - 1)
                mm(banks[a % 2][:, :], xse[:, a % 2, :], w1t[:, e, :], start=True, stop=True).then_inc(s("h_ps"), 1)

            def se_hidden(k, a):
                pe.wait_ge(s("hb_ready"), k + 1)
                reach(pe, s("ht_sb"), k - 1)
                for c in range(FC):
                    last = nc.tensor.transpose(banks[2 + a % 2][:, c * P:(c + 1) * P], hb[:, a % 2, c * P:(c + 1) * P],
                                               ident[:, :])
                last.then_inc(s("ht_ps"), 1)

            def se_down(k, a, e):
                pe.wait_ge(s("ht_sb"), k + 1)
                reach(pe, s("yb_done"), k - 1)
                for c in range(FC):
                    last = mm(banks[4 + a % 2][:, 0:D], ht[:, a % 2, c * P:(c + 1) * P], w2t[:, e, c, :],
                              start=(c == 0), stop=(c == FC - 1))
                last.then_inc(s("ye_ps"), 1)

            def expert_round(i, e, first=False, last=False):
                for a in range(RING):
                    k = RING * i + a
                    if not last or a < RING - 1:
                        se_up(k + 1, (a + 1) % RING, e[a + 2])
                    if not last or a < RING - 3:
                        se_trans(k + 3, (a + 3) % RING, i + (a + 3) // RING)
                    if not (first and a == 0):
                        se_down(k - 1, (a - 1) % RING, e[a])
                    se_hidden(k, a)

            se_trans(0, 0, 0)
            se_trans(1, 1, 0)
            regs = expert_registers(pe)
            e = load_experts(pe, regs, 0)
            se_up(0, 0, e[1])
            se_trans(2, 2, 0)
            expert_round(0, e, first=True)
            with pe.Fori(1, ROUNDS - 1, 1) as i:
                expert_round(i, load_experts(pe, regs, i))
            e = load_experts(pe, regs, ROUNDS - 1)
            expert_round(ROUNDS - 1, e, last=True)
            se_down(NS - 1, RING - 1, e[RING])


_INS = ["L0_attn_x", "L0_attn_W_qkv", "L0_attn_W_o", "L0_ffn_centroids", "L0_ffn_ln_g", "L0_ffn_ln_b", "L0_ffn_w1",
        "L0_ffn_b1", "L0_ffn_w2", "L0_ffn_b2"]


def kernel(**inputs):
    import numpy as _np
    import concourse.bacc as _bacc
    from concourse import mybir as _mybir
    from concourse.bass_utils import run_bass_kernel_spmd as _run

    nc = _bacc.Bacc("TRN2", target_bir_lowering=False, num_devices=1)
    arrays, args = {}, []
    for name in _INS:
        a = _np.ascontiguousarray(inputs[name])
        arrays[f"in_{name}_dram"] = a
        args.append(nc.dram_tensor(f"in_{name}_dram", a.shape, _mybir.dt.from_np(a.dtype), kind="ExternalInput").ap())
    args.append(nc.dram_tensor("out_dram", inputs["L0_attn_x"].shape, _mybir.dt.from_np(_np.dtype("float32")),
                               kind="ExternalOutput").ap())
    moe_attention_kernel(nc, *args)
    r = _run(nc, [arrays], core_ids=[0])
    return r.results[0]["out_dram"]
```

```python
import concourse.bass as bass
from concourse import mybir
from contextlib import ExitStack

F32, F32R, F16, BF16 = mybir.dt.float32, mybir.dt.float32r, mybir.dt.float16, mybir.dt.bfloat16
I32, U32 = mybir.dt.int32, mybir.dt.uint32
ALU = mybir.AluOpType
ACT = mybir.ActivationFunctionType
AX = mybir.AxisListType.X


def reach(eng, sem, value):
    if isinstance(value, int) and value <= 0:
        return
    eng.wait_ge(sem, value)


def reach_alone(eng, sem, value, passed):
    if isinstance(value, int) and value <= 0:
        return
    eng.wait_ge(sem, value)
    if not isinstance(value, int):
        eng.sem_inc(passed, 1)


def moe_attention_kernel(nc, x, w_qkv, w_o, centroids, ln_g, ln_b, w1, b1, w2, b2, out):
    B, L, D = x.shape
    E, F, _ = w1.shape
    P = 128
    H = 16
    DK = D // H
    NCH = L // P
    NT = B * NCH
    NTOK = B * L
    HALF = B // 2
    NQ = NT // HALF
    G = P // 32
    J = H // G
    FC = F // P
    NS = NT + E
    ROW = D + 4
    RING = 8
    ROUNDS = NS // RING
    EPS = 1e-5
    QTOP = 1024.0
    TINY = 1e-30

    x_v = x.rearrange("b (c p) d -> p c b d", p=P)
    slots_d = nc.dram_tensor("slots_d", (NS * P, ROW), F32, kind="Internal").ap()
    out_v = out.rearrange("b (c p) d -> p c b d", p=P)
    slots_v = slots_d.rearrange("(k p) r -> p k r", p=P)
    out_rows = out.rearrange("b l d -> (b l) d")

    ctx = ExitStack()
    with ctx:
        def sb(name, shape, dt=F32):
            return ctx.enter_context(nc.sbuf_tensor(name, shape, dt))

        def sem(name):
            return ctx.enter_context(nc.semaphore(name))

        resid = sb("resid", [P, NT, D])
        first_owner = ExitStack()
        w1t = first_owner.enter_context(nc.sbuf_tensor("w1t", [P, E, F], F32, side="right"))
        rows = first_owner.enter_context(nc.sbuf_tensor("rows", [P, NT, ROW], F32, side="right"))
        first_owner.close()
        w1l = ctx.enter_context(nc.sbuf_tensor("w1l", [P, E, F], F32R, side="right"))
        w1h = ctx.enter_context(nc.sbuf_tensor("w1h", [P, E, F], F32R, side="right"))
        b1b = sb("b1b", [P, E, F])
        w2t = sb("w2t", [P, E, FC, D])
        b2b = sb("b2b", [P, E, D])
        pos_i = sb("pos_i", [P, NT], I32)
        eid_i = sb("eid_i", [P, NS + RING], I32)
        wqkv = sb("wqkv", [P, 3 * D])
        wo = sb("wo", [P, D])
        ident = sb("ident", [P, P])
        identh = sb("identh", [P, P], F16)
        causal = sb("causal", [P, P])
        headmask = sb("headmask", [P, P])
        eps = sb("eps", [P, 1])
        ones = sb("ones", [P, P])
        zrow = sb("zrow", [P, ROW])

        stats = sb("stats", [P, 2, B, 6])
        mv = sb("mv", [P, 2, B, 2])
        std = sb("std", [P, 2, B])
        rs_s = sb("rs_s", [P, 2, B])
        cen_t = sb("cen_t", [P, 32])
        g_t = sb("g_t", [P, E])
        lb_t = sb("lb_t", [P, E])
        var_all = sb("var_all", [P, NT])
        rstd_all = sb("rstd_all", [P, NT])
        mx = sb("mx", [P, NT])
        tmp_nt = sb("tmp_nt", [P, NT])
        tmp_nt2 = sb("tmp_nt2", [P, NT])
        pr = sb("pr", [P, G, J * P])
        pr_v = pr[:, :, :].rearrange("p g (j t) -> p g j t", j=J)
        xq = sb("xq", [P, 2, HALF, ROW])
        xt = sb("xt", [P, HALF, P])
        q32 = sb("q32", [P, HALF * D])
        kv32 = sb("kv32", [P, 4, HALF * D])
        k32, v32 = kv32[:, 0:2, :], kv32[:, 2:4, :]
        sq = sb("sq", [P, HALF * D])
        kvar = sb("kvar", [P, HALF * H])
        kstd = sb("kstd", [P, HALF * H])
        krs = sb("krs", [P, HALF * H])
        qs = sb("qs", [P, 2, HALF * H, 4, DK], F16)
        ks = sb("ks", [P, 2, HALF * H, 4, DK], F16)
        qqt = sb("qqt", [P, 2, J, P], F16)
        kkt = sb("kkt", [P, 2, J, P], F16)
        qt = sb("qt", [P, 2, HALF, P])
        vz = sb("vz", [P, 2, J, P])
        y = sb("y", [P, 2, P])
        state = sb("state", [P, B, P])
        dstate = sb("dstate", [P, HALF, P])
        res = sb("res", [P, 2, HALF, D])
        idxq = sb("idxq", [P, 2, HALF], I32)

        lnx = kv32[:, :, :].rearrange("p a n -> p (a n)").rearrange("p (a b d) -> p a b d", a=2, b=B)
        xta = vz

        def vz_heads(a):
            return bass.AP(tensor=vz, offset=a * J * P, ap=[[2 * J * P, P], [P + DK, J], [32, G], [1, DK]])

        afft = q32[:, :]

        wraw = sq[:, 0:3 * D]
        bound = mx[:, 0:H]

        aff = pr[:, 0, :].rearrange("p (t e) -> p t e", e=E)
        rt1 = pr[:, 1, :].rearrange("p (t e) -> p t e", e=E)
        rt2 = pr[:, 2, :].rearrange("p (t e) -> p t e", e=E)
        scan = pr[:, 3, :].bitcast(BF16).rearrange("p (a t e) -> p a t e", a=2, e=E)
        eidf = res[:, :, :, :].rearrange("p a b d -> p (a b d)")[:, 0:NS * E].rearrange("p (k e) -> p k e", e=E)
        ohb = sb("ohb", [P, NT, E], BF16)
        notbefore = sb("notbefore", [P, P], BF16)
        onesb = sb("onesb", [P, P], BF16)
        desc = sb("desc", [P, E])
        iot_i = sb("iot_i", [P, NS], I32)
        iotk = sb("iotk", [P, NS])
        cnt = sb("cnt", [P, 5, E])
        id_i = sb("id_i", [P, NT], I32)

        w1raw = state[:, :, :].rearrange("p (a c) d -> p a c d", a=2)
        w2raw = res[:, :, :, :].rearrange("p a b d -> p a (b d)")
        lent = qs[:, :, :, :, :].rearrange("p a h r d -> p (a h r d)").bitcast(F32)
        b1row = [dstate[0:1, :, :].rearrange("p a b -> p (a b)"), lent[0:1, 0:F]]
        w1tr = xt[:, :, :].rearrange("p a b -> p (a b)")
        lbb = lent[:, F:F + P]

        xs = sb("xs", [P, RING, ROW])
        xse = sb("xse", [P, 2, 2, P], F32R)
        hb, ht = pr[:, 0:2, :], pr[:, 2:4, :]
        idxe = sb("idxe", [P, RING], I32)
        ye = qs[:, 0, :, :, :].rearrange("p h r d -> p (h r d)").bitcast(F32).rearrange("p (k d) -> p k d", d=D)
        yb = sb("yb", [P, 2, D])

        banks = [ctx.enter_context(nc.psum_tensor(f"bank{i}", [P, 512], F32)) for i in range(8)]

        S = {}

        def bcast(v, axis, n):
            shape = list(v.shape)
            return v.unsqueeze(axis).to_broadcast(shape[:axis] + [n] + shape[axis:])

        def s(name):
            if name not in S:
                S[name] = sem(name)
            return S[name]

        block = ctx.enter_context(nc.Block())

        def expert_registers(eng):
            return [eng.alloc_register(f"expert{j}") for j in range(RING + 3)]

        def load_experts(eng, regs, i):
            eng.load(regs, eid_i[0:1, bass.ds(RING * i, RING + 3)])
            return [eng.snap(r, min_val=0, max_val=E - 1) for r in regs]

        SC = [banks[0], banks[1]]
        YB, QB, KB, CB, EB, DB = banks[2], banks[3], banks[4], banks[5], banks[6], banks[7]
        qb16 = QB[:, 0:256].bitcast(F16).rearrange("p (j t) -> p j t", j=J)
        kb16 = KB[:, 0:256].bitcast(F16).rearrange("p (j t) -> p j t", j=J)

        @block.sync
        def _(sp):
            sp.dma_start(wraw, w_qkv).then_inc(s("wqkv_in"), 16)
            sp.dma_start(wo[:, :], w_o).then_inc(s("wo_in"), 16)

            def load_x(c, a):
                reach(sp, s("stats_done"), c - 1)
                sp.dma_start(resid[:, bass.ds(c * B, B), :], x_v[:, c, :, :]).then_inc(s(f"x_in{a}"), 16)

            def load_expert(e, a):
                reach(sp, s("b1_ps"), e - 1)
                sp.dma_start(w1raw[:, a, :, :], w1.rearrange("e (c p) d -> p e c d", p=P)[:, e, :, :])\
                  .then_inc(s(f"wraw_in{a}"), 16)
                sp.dma_start(w2raw[:, a, :], w2.rearrange("e d f -> d e f")[:, e, :]).then_inc(s(f"wraw_in{a}"), 16)
                sp.dma_start(b1row[a], b1.rearrange("(o e) f -> o e f", o=1)[:, e, :])\
                  .then_inc(s(f"wraw_in{a}"), 16)

            for c in range(2):
                load_x(c, c)
            for e in range(2):
                load_expert(e, e)
            for c in range(2, 5):
                load_x(c, c % 2)
            for e in range(2, E):
                load_expert(e, e % 2)
                if e + 3 < NCH:
                    load_x(e + 3, (e + 3) % 2)

            def store_quad(n, c, half):
                sp.wait_ge(s("res_ready"), n + 1)
                sp.dma_start(out_v[:, c, half * HALF:(half + 1) * HALF, :], res[:, half, :, :])\
                  .then_inc(s(f"attn_out{half}"), 16)

            def load_slots(k, a):
                reach(sp, s("ye_ready"), k - RING + 1)
                sp.dma_start(xs[:, a, :], slots_v[:, k, :]).then_inc(s(f"se_in{a}"), 16)

            with sp.Fori(0, NCH - 1, 1) as c:
                for half in range(2):
                    store_quad(2 * c + half, c, half)
            store_quad(NQ - 2, NCH - 1, 0)
            for half in range(2):
                sp.wait_ge(s(f"scattered{half}"), 16 * HALF * NCH)
            for a in range(RING):
                load_slots(a, a)
            store_quad(NQ - 1, NCH - 1, 1)
            with sp.Fori(1, ROUNDS, 1) as i:
                for a in range(RING):
                    load_slots(RING * i + a, a)
            for a in range(RING):
                sp.wait_ge(s(f"out_done{a}"), 16 * ROUNDS)

        @block.gpsimd
        def _(pool):
            pool.memset(ident[:, :], 0.0).then_inc(s("pool_c"), 1)
            pool.memset(causal[:, :], 1.0).then_inc(s("pool_c"), 1)
            pool.memset(headmask[:, :], 1.0).then_inc(s("pool_c"), 1)
            pool.memset(rt1[:, :, :], 1.0).then_inc(s("pool_c"), 1)
            pool.memset(zrow[:, :], 0.0).then_inc(s("pool_c"), 1)
            pool.wait_ge(s("pool_c"), 5)
            pool.affine_select(out=ident[:, :], in_=ident[:, :], compare_op=ALU.not_equal, fill=1.0, base=0,
                               pattern=[[-1, P]], channel_multiplier=1).then_inc(s("ident_ready"), 1)
            pool.affine_select(out=causal[:, :], in_=causal[:, :], compare_op=ALU.is_ge, fill=0.0, base=0,
                               pattern=[[1, P]], channel_multiplier=-1).then_inc(s("pool_m"), 1)
            hm = headmask[:, :].rearrange("p (g j d) -> p g j d", g=G, d=DK)
            pool.affine_select(out=hm, in_=hm, compare_op=ALU.is_ge, fill=0.0, base=0,
                               pattern=[[-DK, G], [-32, J], [0, DK]], channel_multiplier=1).then_inc(s("pool_m"), 1)
            ones_v = rt1.rearrange("p t e -> p (t e)")
            pool.affine_select(out=ones_v[:, 0:P], in_=ones_v[:, 0:P], compare_op=ALU.is_ge, fill=0.0, base=-1,
                               pattern=[[1, P]], channel_multiplier=-1).then_inc(s("pool_m"), 1)
            pool.wait_ge(s("pool_m"), 2)
            pool.affine_select(out=hm, in_=hm, compare_op=ALU.is_ge, fill=0.0, base=DK - 1,
                               pattern=[[DK, G], [32, J], [0, DK]], channel_multiplier=-1).then_inc(s("pool_m"), 1)
            pool.iota(iot_i[:, :], [[1, NS]], base=0, channel_multiplier=0).then_inc(s("pool_m"), 1)
            pool.iota(id_i[:, :].rearrange("p (c b) -> p c b", b=B), [[-P, NCH], [-L, B]], base=NTOK,
                              channel_multiplier=-1).then_inc(s("pool_m"), 1)
            pool.dma_start(b2b[:, :, :], b2.partition_broadcast(P)).then_inc(s("b2_in"), 16)

            ZERO = NS // NCH

            def add_resid(i, a):
                pool.dma_start(slots_v[:, bass.ds((2 * i + a) * ZERO, ZERO), :], bcast(zrow[:, :], 1, ZERO))\
                    .then_inc(s("slots_zero"), 16)
                pool.wait_ge(s("lnx_ready"), 2 * i + a + 1)
                t0 = (2 * i + a) * B
                pool.tensor_tensor(resid[:, bass.ds(t0, B), :], resid[:, bass.ds(t0, B), :], lnx[:, a, :, :], ALU.add)\
                    .then_inc(s("resid_ready"), 1)

            with pool.Fori(0, NCH // 2, 1) as i:
                for a in range(2):
                    add_resid(i, a)

            def split_high(src, dst, done):
                pool.tensor_scalar(dst, src, 1.0, 0.0, ALU.mult, ALU.add).then_inc(done, 1)

            def q_high(n, par):
                reach_alone(pool, s("q_sb"), n + 1, s("pool_passed"))
                reach_alone(pool, s("qk_ps"), 4 * (n - 1), s("pool_passed"))
                split_high(q32[:, :].rearrange("p (h d) -> p h d", d=DK), qs[:, par, :, 0, :], s("q_hi"))

            def k_high(n, par):
                reach_alone(pool, s("k_sb"), n + 1, s("pool_passed"))
                split_high(k32[:, par, :].rearrange("p (h d) -> p h d", d=DK), ks[:, par, :, 0, :], s("k_hi"))

            def mask_scores(n, i, g):
                reach_alone(pool, s("sc_even"), 8 * n + 2 * i + g // 2 + 1, s("pool_passed"))
                pool.affine_select(out=pr_v[:, g, :, :], in_=pr_v[:, g, :, :], compare_op=ALU.is_ge, fill=0.0, base=0,
                                   pattern=[[0, J], [1, P]], channel_multiplier=-1).then_inc(s("pr_even"), 1)

            def scatter_index(n, c, half):
                if not (isinstance(c, int) and c == 0):
                    pool.wait_ge(s(f"scattered{half}"), 16 * HALF * c)
                pool.tensor_copy(idxq[:, half, :], pos_i[:, bass.ds(c * B + half * HALF, HALF)])\
                    .then_inc(s("idx_ready"), 1)
                reach_alone(pool, s("idx_ready"), n + 1, s("pool_passed"))

            def scatter_rows(i, half):
                pool.indirect_dma_start(slots_d, bass.IndirectOffsetOnAxis(ap=idxq[:, half, i:i + 1], axis=0),
                                        xq[:, half, i, :], None, bounds_check=NS * P - 1, oob_is_err=False)\
                    .then_inc(s(f"scattered{half}"), 16)

            def scatter_quad(n, c, half, i):
                if i == 0:
                    pool.wait_ge(s("xq_ready"), n + 1)
                    scatter_index(n, c, half)
                scatter_rows(i, half)

            def quad(n, c, half, first=False, more=True, ahead=True):
                c_next, other = (c if half == 0 else c + 1), 1 - half
                for i in range(HALF):
                    mask_scores(n, i, 0)
                    if more and i == 2:
                        k_high(n + 1, other)
                    if first and i == 0:
                        pool.wait_ge(s("slots_zero"), 16 * NCH)
                        pool.wait_ge(s("xq_columns"), 1)
                    if first:
                        scatter_quad(0, 0, 0, i)
                    if more:
                        scatter_quad(n + 1, c_next, other, i)
                    mask_scores(n, i, 2)
                    if more and i == 1:
                        q_high(n + 1, other)
                if not ahead:
                    return
                pool.wait_ge(s("ds_sb"), n + 1)
                pool.wait_ge(s("av_ps"), 16 * n + 13)
                pool.tensor_tensor(state[:, half * HALF:(half + 1) * HALF, :], state[:, half * HALF:(half + 1) * HALF, :],
                                   dstate[:, :, :], ALU.add).then_inc(s("state_ready"), 1)

            pool.wait_ge(s("b1_ps"), E)
            pool.memset(state[:, :, :], 0.0).then_inc(s("state_zero"), 1)
            pool.wait_ge(s("aff_ps"), 2 * NCH)
            pool.memset(vz[:, :, :, :], 0.0).then_inc(s("vz_zero"), 1)
            pool.wait_ge(s("state_zero"), 1)
            q_high(0, 0)
            k_high(0, 0)
            quad(0, 0, 0, first=True)
            quad(1, 0, 1)
            with pool.Fori(1, NCH - 1, 1) as c:
                quad(2 * c, c, 0)
                quad(2 * c + 1, c, 1)
            quad(NQ - 2, NCH - 1, 0, ahead=False)
            quad(NQ - 1, NCH - 1, 1, more=False, ahead=False)

            for half in range(2):
                pool.wait_ge(s(f"attn_out{half}"), 16 * NCH)

            def scatter_out(k, a):
                reach_alone(pool, s("ye_ready"), k + 1, s("pool_passed"))
                pool.indirect_dma_start(out_rows, bass.IndirectOffsetOnAxis(ap=idxe[:, a:a + 1].bitcast(U32), axis=0),
                                        ye[:, a, :], None, bounds_check=NTOK - 1, oob_is_err=False,
                                        compute_op=ALU.add)\
                    .then_inc(s(f"out_done{a}"), 16)

            with pool.Fori(0, ROUNDS, 1) as i:
                for a in range(RING):
                    scatter_out(RING * i + a, a)

        @block.scalar
        def _(act):
            act.wait_ge(s("cen_zero"), 1)
            act.dma_start(cen_t[:, 0:E], centroids.rearrange("e d -> d e"), allow_slow_non_contiguous=True)\
                .then_inc(s("cen_in"), 16)
            act.dma_start(g_t[:, :], ln_g.rearrange("e d -> d e"), allow_slow_non_contiguous=True).then_inc(s("lng_in"), 16)
            act.dma_start(lb_t[:, :], ln_b.rearrange("e d -> d e"), allow_slow_non_contiguous=True).then_inc(s("lng_in"), 16)
            act.wait_ge(s("eps_ready"), 1)

            act.wait_ge(s("qbound"), 1)
            nc.scalar.activation(bound, tmp_nt2[:, 0:H], ACT.Sqrt, scale=float(P) / (QTOP * QTOP))\
                .then_inc(s("qbound_root"), 1)

            def ln_root(c, a):
                act.wait_ge(s("mv_ready"), c + 1)
                nc.scalar.activation(std[:, a, :], mv[:, a, :, 1], ACT.Sqrt, bias=eps[:, 0:1]).then_inc(s("std_ready"), 1)

            def ln_copy(c, a):
                for hf in range(2):
                    act.wait_ge(s("xta_ps"), 2 * c + hf + 1)
                    reach(act, s("aff_ps"), 2 * c + hf - 1)
                    nc.scalar.activation(xta[:, hf, :, :], banks[hf][:, :].rearrange("p (a b) -> p a b", a=HALF),
                                         ACT.Copy).then_inc(s("xta_sb"), 1)

            def rows_copy(c, a):
                act.wait_ge(s("lnx_ready"), c + 1)
                nc.scalar.activation(rows[:, bass.ds(c * B, B), 0:D], lnx[:, a, :, :], ACT.Copy)\
                    .then_inc(s("rows_ready"), 1)

            def bias_copy(e):
                act.wait_ge(s("b1_ps"), e + 1)
                nc.scalar.activation(b1b[:, e, :], banks[4][:, :], ACT.Copy).then_inc(s("b1b_ready"), 1)

            def prep(e):
                act.wait_ge(s("w1t_ps"), e + 1)
                nc.scalar.activation(w1tr, banks[2][:, :], ACT.Copy)
                nc.scalar.activation(lbb, ones[:, :], ACT.Copy, scale=lb_t[:, bass.ds(e, 1)]).then_inc(s("w1tr_ready"), 1)
                nc.scalar.activation(w1t[:, e, :], banks[2][:, :], ACT.Copy, scale=g_t[:, bass.ds(e, 1)])\
                    .then_inc(s("w1t_ready"), 1)
                act.wait_ge(s("w2t_ps"), e + 1)
                nc.scalar.activation(w2t[:, e, :, :], banks[3][:, :].rearrange("p (c d) -> p c d", c=FC), ACT.Copy)\
                    .then_inc(s("w2t_ready"), 1)

            def affinity_copy(i):
                act.wait_ge(s("aff_ps"), 4 * (i + 1))
                reach(act, s("aff_t"), i)
                nc.scalar.activation(afft, banks[7][:, :], ACT.Copy).then_inc(s("aff_sb"), 1)

            def chunk(c, a, i, first=False, last=False):
                if not last:
                    ln_root(c + 1, 1 - a)
                ln_copy(c, a)
                if not first:
                    bias_copy(c - 1)
                if a == 1:
                    affinity_copy(i)
                rows_copy(c, a)
                prep(c)

            ln_root(0, 0)
            act.wait_ge(s("lng_in"), 32)
            chunk(0, 0, 0, first=True)
            chunk(1, 1, 0)
            with act.Fori(1, NCH // 2 - 1, 1) as i:
                for a in range(2):
                    chunk(2 * i + a, a, i)
            chunk(NCH - 2, 0, NCH // 2 - 1)
            chunk(NCH - 1, 1, NCH // 2 - 1, last=True)

            act.wait_ge(s("var2_ready"), 1)
            nc.scalar.activation(tmp_nt2[:, :], tmp_nt[:, :], ACT.Sqrt, bias=eps[:, 0:1]).then_inc(s("std2_ready"), 1)

            def x_transposed(n):
                act.wait_ge(s("xt_ps"), n + 1)
                reach(act, s("v_ps"), n)
                nc.scalar.activation(xt[:, :, :].rearrange("p a b -> p (a b)"), EB[:, :], ACT.Copy).then_inc(s("xt_sb"), 1)

            def q_copy(n):
                act.wait_ge(s("q_ps"), n + 1)
                reach(act, s("q_lo"), n)
                reach(act, s("qt_ps"), n)
                nc.scalar.activation(q32[:, :], CB[:, :], ACT.Copy).then_inc(s("q_sb"), 1)

            def k_square(n):
                act.wait_ge(s("k_ps"), n + 1)
                reach(act, s("kvar_ready"), n)
                nc.scalar.activation(sq[:, :], EB[:, :], ACT.Square).then_inc(s("sq_ready"), 1)

            def k_root(n):
                act.wait_ge(s("kvar_ready"), n + 1)
                reach(act, s("k_sb"), n)
                nc.scalar.activation(kstd[:, :], kvar[:, :], ACT.Sqrt, scale=1.0 / DK, bias=eps[:, 0:1])\
                    .then_inc(s("kstd_ready"), 1)

            def v_copy(n, par):
                act.wait_ge(s("v_ps"), n + 1)
                reach(act, s("ds_ps"), n - 1)
                nc.scalar.activation(v32[:, par, :], CB[:, :], ACT.Copy).then_inc(s("v_sb"), 1)

            def q_transposed(n, par):
                act.wait_ge(s("qt_ps"), n + 1)
                reach(act, s("av_ps"), 16 * (n - 1))
                nc.scalar.activation(qt[:, par, :, :].rearrange("p a b -> p (a b)"), EB[:, :], ACT.Copy).then_inc(s("qt_sb"), 1)

            def qq_copy(m, a):
                act.wait_ge(s("qk_ps"), m + 1)
                reach(act, s("sc_ps"), 4 * (m - 1))
                nc.scalar.activation(qqt[:, a, :, :], qb16, ACT.Copy).then_inc(s("qq_sb"), 1)

            def score_copy(m, g):
                act.wait_ge(s("sc_ps"), 4 * m + g + 1)
                reach(act, s("av_ps"), 4 * (m - 1) + g + 1)
                nc.scalar.activation(pr[:, g, :], SC[0][:, :], ACT.Copy).then_inc(s("sc_even"), 1)

            def y_copy(m, a):
                act.wait_ge(s("av_ps"), 4 * m + 4)
                reach(act, s("out_ps"), m - 1)
                nc.scalar.activation(y[:, a, :], YB[:, 0:P], ACT.Copy).then_inc(s("y_sb"), 1)

            def w1_high(e):
                act.wait_ge(s("xq_ready"), NQ)
                nc.scalar.activation(w1h[:, e, :], w1t[:, e, :], ACT.Copy).then_inc(s("w1_hi"), 1)

            def quad(n, c, half, first=False, more=True):
                for i in range(HALF):
                    m = 4 * n + i
                    score_copy(m, 0)
                    if not (first and i == 0):
                        y_copy(m - 1, (i + 1) % 2)
                    if more and i == 0:
                        x_transposed(n + 1)
                    if more or i < 3:
                        qq_copy(m + 1, (i + 1) % 2)
                    if more and i == 1:
                        q_copy(n + 1)
                    if more and i == 2:
                        v_copy(n + 1, 1 - half)
                    score_copy(m, 2)
                    if more and i == 0:
                        k_square(n + 1)
                    if more and i == 1:
                        k_root(n + 1)
                    if more and i == 2:
                        q_transposed(n + 1, 1 - half)
                    if isinstance(c, int) and c == NCH - 1:
                        w1_high(HALF * half + i)

            act.wait_ge(s("resid_ready"), NCH)
            act.wait_ge(s("xta_ps"), 2 * NCH)
            bias_copy(E - 1)
            x_transposed(0)
            q_copy(0)
            k_square(0)
            k_root(0)
            v_copy(0, 0)
            q_transposed(0, 0)
            act.wait_ge(s("mx_ready"), 1)
            nc.scalar.activation(rows[:, :, D + 1], mx[:, :], ACT.Sigmoid).then_inc(s("gate_ready"), 1)
            qq_copy(0, 0)
            quad(0, 0, 0, first=True)
            quad(1, 0, 1)
            with act.Fori(1, NCH - 1, 1) as c:
                quad(2 * c, c, 0)
                quad(2 * c + 1, c, 1)
            quad(NQ - 2, NCH - 1, 0)
            quad(NQ - 1, NCH - 1, 1, more=False)
            y_copy(NT - 1, 1)

            def se_x(k, a):
                act.wait_ge(s("sex_ps"), k + 1)
                reach(act, s("h_ps"), k - 1)
                nc.scalar.activation(xse[:, a % 2, 0, :], banks[6 + a % 2][:, 0:P], ACT.Copy).then_inc(s("sex_sb"), 1)

            def se_relu(k, a):
                act.wait_ge(s("ht_ps"), k + 1)
                reach(act, s("ye_ps"), k - 1)
                nc.scalar.activation(ht[:, a % 2, :], banks[2 + a % 2][:, :], ACT.Relu).then_inc(s("ht_sb"), 1)

            se_x(0, 0)
            se_x(1, 1)
            se_x(2, 0)
            for k in range(2):
                se_x(k + 3, 1 - k)
                se_relu(k, k)
            with act.Fori(1, NS // 2 - 2, 1) as i:
                for a in range(2):
                    se_x(2 * i + a + 3, 1 - a)
                    se_relu(2 * i + a, a)
            se_x(NS - 1, 1)
            for k in range(NS - 4, NS):
                se_relu(k, k % 2)

        @block.vector
        def _(dve):
            chain = [0]

            def link(ins):
                chain[0] += 1
                ins.then_inc(s("dve_chain"), 1)
                dve.wait_ge(s("dve_chain"), chain[0])

            nc.vector.memset(cen_t[:, :], 0.0).then_inc(s("cen_zero"), 1)
            nc.vector.memset(eps[:, :], EPS).then_inc(s("eps_ready"), 1)
            nc.vector.memset(ones[:, :], 1.0).then_inc(s("ones_ready"), 1)
            nc.vector.memset(onesb[:, :], 1.0)
            nc.vector.memset(eid_i[:, 0:2], 0)
            nc.vector.memset(eid_i[:, NS + 2:NS + RING], 0)
            for e in range(E):
                nc.vector.memset(desc[:, e:e + 1], float(E - e))

            dve.wait_ge(s("pool_m"), 6)
            ones_v = rt1.rearrange("p t e -> p (t e)")
            nc.vector.tensor_scalar(notbefore[:, :], ones_v[:, 0:P], 1.0, None, ALU.subtract)
            nc.vector.tensor_copy(iotk[:, :], iot_i[:, :])

            dve.wait_ge(s("wqkv_in"), 16)
            for part in range(2):
                nc.vector.tensor_copy(wqkv[:, part * D:(part + 1) * D].rearrange("p (j g d) -> p j g d", j=J, g=G),
                                      wraw[:, part * D:(part + 1) * D].rearrange("p (g j d) -> p j g d", j=J, g=G))
            link(nc.vector.tensor_copy(wqkv[:, 2 * D:3 * D], wraw[:, 2 * D:3 * D]))
            wk = wqkv[:, D:2 * D].rearrange("p (h d) -> p h d", d=DK)
            link(nc.vector.tensor_reduce(out=tmp_nt[:, 0:H], in_=wk, axis=AX, op=ALU.add))
            link(nc.vector.tensor_scalar(tmp_nt[:, 0:H], tmp_nt[:, 0:H], 1.0 / DK, None, ALU.mult))
            nc.vector.tensor_tensor(wk, wk, bcast(tmp_nt[:, 0:H], 2, DK),
                                    ALU.subtract)
            nc.vector.tensor_tensor(sq[:, 0:D], wqkv[:, 0:D], wqkv[:, 0:D], ALU.mult).then_inc(s("wq_sq"), 1)
            def ln_stats(i, a):
                c = 2 * i + a
                dve.wait_ge(s(f"x_in{a}"), 16 * (i + 1))
                for b in range(B):
                    last = nc.vector.bn_stats(stats[:, a, b, :], resid[:, c * B + b, :])
                last.then_inc(s("stats_done"), 1)
                reach_alone(dve, s("stats_done"), c + 1, s("dve_passed"))
                for b in range(B):
                    last = nc.vector.bn_aggr(mv[:, a, b, :], stats[:, a, b, :])
                last.then_inc(s("mv_ready"), 1)

            def ln_norm(c, a):
                dve.wait_ge(s("mv_ready"), c + 1)
                nc.vector.tensor_copy(var_all[:, bass.ds(c * B, B)], mv[:, a, :, 1])
                dve.wait_ge(s("std_ready"), c + 1)
                nc.vector.reciprocal(rs_s[:, a, :], std[:, a, :]).then_inc(s("rs_done"), 1)
                reach(dve, s("xta_ps"), 2 * (c - 1))
                reach(dve, s("resid_ready"), c - 1)
                reach(dve, s("rows_ready"), c - 1)
                dve.wait_ge(s("rs_done"), c + 1)
                nc.vector.tensor_copy(rstd_all[:, bass.ds(c * B, B)], rs_s[:, a, :])
                for b in range(B):
                    last = nc.vector.tensor_scalar(lnx[:, a, b, :], resid[:, c * B + b, :], mv[:, a, b, 0:1],
                                                   rs_s[:, a, b:b + 1], ALU.subtract, ALU.mult)
                last.then_inc(s("lnx_ready"), 1)

            def affinity_in(i):
                dve.wait_ge(s("aff_t"), i + 1)
                nc.vector.tensor_copy(aff[:, bass.ds(2 * B * i, 2 * B), :].rearrange("p (g b) e -> p b g e", b=HALF),
                                      banks[5][:, :].rearrange("p (b g r) -> p b g r", b=HALF, g=G)[:, :, :, 0:E])\
                    .then_inc(s("aff_in"), 1)

            def chunk(i, a, first=False):
                ln_stats(i if a == 0 else i + 1, 1 - a)
                ln_norm(2 * i + a, a)
                if a == 1 and not first:
                    affinity_in(i - 1)

            ln_stats(0, 0)
            dve.wait_ge(s("norm_ps"), 1)
            nc.vector.tensor_reduce(out=tmp_nt2[:, 0:H], in_=banks[6][:, 0:D].rearrange("p (h d) -> p h d", d=DK),
                                    axis=AX, op=ALU.max).then_inc(s("qbound"), 1)
            dve.wait_ge(s("qbound_root"), 1)
            link(nc.vector.tensor_scalar(bound, bound, TINY, None, ALU.max))
            link(nc.vector.reciprocal(tmp_nt[:, H:2 * H], bound))
            wq = wqkv[:, 0:D].rearrange("p (h d) -> p h d", d=DK)
            nc.vector.tensor_tensor(wq, wq, bcast(tmp_nt[:, H:2 * H], 2, DK),
                                    ALU.mult).then_inc(s("wqkv_ready"), 1)
            ln_stats(0, 1)
            ln_norm(0, 0)
            chunk(0, 1, first=True)
            with dve.Fori(1, NCH // 2 - 1, 1) as i:
                for a in range(2):
                    chunk(i, a)
            chunk(NCH // 2 - 1, 0)
            ln_norm(NCH - 1, 1)
            affinity_in(NCH // 2 - 2)

            def x_copy(n, c, half, columns=ROW):
                reach(dve, s("xt_ps"), n - 1)
                if not (isinstance(c, int) and c == 0):
                    dve.wait_ge(s(f"scattered{half}"), 16 * HALF * c)
                nc.vector.tensor_copy(xq[:, half, :, 0:columns],
                                      rows[:, bass.ds(c * B + half * HALF, HALF), 0:columns]).then_inc(s("xq_ready"), 1)

            def k_var(n):
                dve.wait_ge(s("sq_ready"), n + 1)
                nc.vector.tensor_reduce(out=kvar[:, :], in_=sq[:, :].rearrange("p (h d) -> p h d", d=DK), axis=AX,
                                        op=ALU.add).then_inc(s("kvar_ready"), 1)

            def k_norm(n, par):
                dve.wait_ge(s("kstd_ready"), n + 1)
                nc.vector.reciprocal(krs[:, :], kstd[:, :]).then_inc(s("krs_ready"), 1)
                dve.wait_ge(s("krs_ready"), n + 1)
                reach(dve, s("ds_ps"), n - 1)
                nc.vector.tensor_tensor(k32[:, par, :].rearrange("p (h d) -> p h d", d=DK),
                                        EB[:, :].rearrange("p (h d) -> p h d", d=DK),
                                        bcast(krs[:, :], 2, DK), ALU.mult)\
                    .then_inc(s("k_sb"), 1)

            def q_low(n, par):
                dve.wait_ge(s("q_hi"), n + 1)
                nc.vector.tensor_tensor(qs[:, par, :, 2, :], q32[:, :].rearrange("p (h d) -> p h d", d=DK),
                                        qs[:, par, :, 0, :], ALU.subtract).then_inc(s("q_lo"), 1)
                dve.wait_ge(s("q_lo"), n + 1)
                nc.vector.tensor_copy(qs[:, par, :, 1::2, :], qs[:, par, :, 0::2, :]).then_inc(s("q_parts"), 1)

            def k_low(n, par):
                dve.wait_ge(s("k_hi"), n + 1)
                nc.vector.tensor_tensor(ks[:, par, :, 1, :], k32[:, par, :].rearrange("p (h d) -> p h d", d=DK),
                                        ks[:, par, :, 0, :], ALU.subtract).then_inc(s("k_lo"), 1)
                dve.wait_ge(s("k_lo"), n + 1)
                nc.vector.tensor_copy(ks[:, par, :, 2:4, :], ks[:, par, :, 0:2, :]).then_inc(s("k_parts"), 1)

            def kk_copy(m, a):
                dve.wait_ge(s("qk_ps"), m + 1)
                reach(dve, s("sc_ps"), 4 * (m - 1))
                nc.vector.tensor_copy(kkt[:, a, :, :], kb16).then_inc(s("kk_sb"), 1)

            def score_mask(m, g):
                dve.wait_ge(s("sc_ps"), 4 * m + g + 1)
                reach(dve, s("av_ps"), 4 * (m - 1) + g + 1)
                nc.vector.tensor_tensor(pr_v[:, g, :, :], SC[1][:, :].rearrange("p (j t) -> p j t", j=J),
                                        bcast(causal[:, :], 1, J), ALU.mult)\
                    .then_inc(s("pr_odd"), 1)

            def v_heads(m, n, i, par):
                dve.wait_ge(s("v_sb"), n + 1)
                reach(dve, s("av_ps"), 4 * (m - 1))
                nc.vector.tensor_copy(vz_heads(i % 2), v32[:, par, i * D:(i + 1) * D]
                                      .rearrange("p (g j d) -> p j g d", g=G, j=J)).then_inc(s("vz_ready"), 1)

            def dstate_mask(n):
                dve.wait_ge(s("ds_ps"), n + 1)
                reach(dve, s("state_ready"), n)
                nc.vector.tensor_tensor(dstate[:, :, :], CB[:, :].rearrange("p (a b) -> p a b", a=HALF),
                                        bcast(headmask[:, :], 1, HALF), ALU.mult)\
                    .then_inc(s("ds_sb"), 1)

            def result(n, c, half):
                dve.wait_ge(s("out_ps"), 4 * n + 4)
                if not (isinstance(c, int) and c == 0):
                    dve.wait_ge(s(f"attn_out{half}"), 16 * c)
                nc.vector.tensor_tensor(res[:, half, :, :], DB[:, :].rearrange("p (a b) -> p a b", a=HALF),
                                        resid[:, bass.ds(c * B + half * HALF, HALF), :], ALU.add)\
                    .then_inc(s("res_ready"), 1)

            def quad(n, c, half, first=False, more=True, ahead=True):
                other = 1 - half
                for i in range(HALF):
                    m = 4 * n + i
                    if more or i < 3:
                        kk_copy(m + 1, (i + 1) % 2)
                    if more and i == 1:
                        k_var(n + 1)
                    score_mask(m, 1)
                    if more and i == 2:
                        q_low(n + 1, other)
                    if ahead and i == 3:
                        dstate_mask(n)
                    score_mask(m, 3)
                    if more and i == 1:
                        k_norm(n + 1, other)
                    if not first and i == 0:
                        result(n - 1, c if half == 1 else c - 1, other)
                    if more and i == 2:
                        k_low(n + 1, other)
                    if i < 3:
                        v_heads(m + 1, n, i + 1, half)
                    elif more:
                        v_heads(m + 1, n + 1, 0, other)
                    if ahead and i == 3:
                        x_copy(n + 2, c + 1, half)
                    if not ahead:
                        w1_low(HALF * half + i)
            def w1_low(e):
                dve.wait_ge(s("w1_hi"), e + 1)
                nc.vector.tensor_tensor(w1l[:, e, :], w1t[:, e, :], w1h[:, e, :].bitcast(F32), ALU.subtract)\
                    .then_inc(s("w1_lo"), 1)

            def over_e(v):
                return bcast(v, 2, E)

            def over_t(v, n=NT):
                return bcast(v, 1, n)

            dve.wait_ge(s("rows_ready"), 1)
            x_copy(0, 0, 0, D)
            x_copy(1, 0, 1, D)
            dve.wait_ge(s("lnx_ready"), NCH)
            link(nc.vector.tensor_tensor(tmp_nt[:, :], rstd_all[:, :], rstd_all[:, :], ALU.mult))
            nc.vector.tensor_tensor(tmp_nt[:, :], tmp_nt[:, :], var_all[:, :], ALU.mult).then_inc(s("var2_ready"), 1)
            dve.wait_ge(s("ident_ready"), 1)
            dve.wait_ge(s("wo_in"), 16)
            per = sq[:, D:2 * D].rearrange("p (h d) -> p h d", d=DK)
            idv = ident[:, :].rearrange("p (h d) -> p h d", d=DK)
            for g in range(G):
                last = nc.vector.tensor_tensor(per[:, J * g:J * (g + 1), :], idv[:, J * g:J * (g + 1), :],
                                               bcast(bound[:, g:H:G], 2, DK), ALU.mult)
            link(last)
            link(nc.vector.tensor_reduce(out=cnt[:, 0, 0:1], in_=sq[:, D:2 * D], axis=AX, op=ALU.add))
            link(nc.vector.tensor_scalar(wo[:, :], wo[:, :], cnt[:, 0, 0:1], None, ALU.mult))
            nc.vector.tensor_copy(identh[:, :], ident[:, :]).then_inc(s("wo_ready"), 1)

            affinity_in(NCH // 2 - 1)
            dve.wait_ge(s("aff_in"), NCH // 2)
            nc.vector.tensor_reduce(out=mx[:, :], in_=aff, axis=AX, op=ALU.max).then_inc(s("mx_ready"), 1)
            dve.wait_ge(s("mx_ready"), 1)
            link(nc.vector.tensor_tensor(rt2, aff, over_e(mx[:, :]), ALU.is_ge))
            link(nc.vector.tensor_tensor(rt2, rt2, over_t(desc[:, :]), ALU.mult))
            link(nc.vector.tensor_reduce(out=rstd_all[:, :], in_=rt2, axis=AX, op=ALU.max))
            link(nc.vector.tensor_tensor(ohb[:, :, :], rt2, over_e(rstd_all[:, :]), ALU.is_equal))
            cur, nxt = ohb[:, :, :], scan[:, 0, :, :]
            spare = scan[:, 1, :, :]
            step = 1
            while step < NT:
                nc.vector.tensor_copy(nxt[:, 0:step, :], cur[:, 0:step, :])
                ins = nc.vector.tensor_tensor(nxt[:, step:NT, :], cur[:, step:NT, :], cur[:, 0:NT - step, :], ALU.add)
                cur, nxt = nxt, (spare if step == 1 else cur)
                step *= 2
                if step < NT:
                    link(ins)
            ins.then_inc(s("scan_ready"), 1)
            k_var(0)
            dve.wait_ge(s("std2_ready"), 1)
            nc.vector.reciprocal(rows[:, :, D], tmp_nt2[:, :])
            nc.vector.tensor_copy(rows[:, :, D + 2], id_i[:, :])
            nc.vector.memset(rows[:, :, D + 3], 0.0)
            dve.wait_ge(s("resid_ready"), NCH)
            dve.wait_ge(s("rows_ready"), NCH)
            k_norm(0, 0)
            tiles_cmp = aff.rearrange("p t e -> p (t e)").rearrange("p (e k) -> p e k", e=E)
            dve.wait_ge(s("rank_ps"), 2)
            link(nc.vector.tensor_scalar(cnt[:, 0, :], banks[1][:, 0:E], 1.0 / P, None, ALU.mult))
            link(nc.vector.tensor_tensor(tiles_cmp, bcast(cnt[:, 0, :], 2, NT),
                                         over_t(iotk[:, 0:NT], E), ALU.is_gt))
            link(nc.vector.tensor_reduce(out=cnt[:, 1, :], in_=tiles_cmp, axis=AX, op=ALU.add))
            link(nc.vector.tensor_copy(cnt[:, 2, :], cnt[:, 1, :]))
            a_, b_ = 2, 3
            step = 1
            while step < E:
                nc.vector.tensor_copy(cnt[:, b_, 0:step], cnt[:, a_, 0:step])
                link(nc.vector.tensor_tensor(cnt[:, b_, step:E], cnt[:, a_, step:E], cnt[:, a_, 0:E - step], ALU.add))
                a_, b_ = b_, a_
                step *= 2
            link(nc.vector.tensor_tensor(cnt[:, 4, :], cnt[:, a_, :], cnt[:, 1, :], ALU.subtract))
            link(nc.vector.tensor_scalar(cnt[:, 4, :], cnt[:, 4, :], float(P), None, ALU.mult))
            q_low(0, 0)
            k_low(0, 0)
            link(nc.vector.tensor_tensor(rt2, banks[0][:, :].rearrange("p (t e) -> p t e", e=E), over_t(cnt[:, 4, :]),
                                         ALU.add))
            link(nc.vector.tensor_tensor(rt2, rt2, ohb[:, :, :], ALU.mult))
            link(nc.vector.tensor_reduce(out=tmp_nt[:, :], in_=rt2, axis=AX, op=ALU.add))
            nc.vector.tensor_copy(pos_i[:, :], tmp_nt[:, :]).then_inc(s("route_done"), 1)
            kk_copy(0, 0)
            dve.wait_ge(s("vz_zero"), 1)
            v_heads(0, 0, 0, 0)
            dve.wait_ge(s("gate_ready"), 1)
            for half in range(2):
                last = nc.vector.tensor_copy(xq[:, half, :, D:ROW], rows[:, half * HALF:(half + 1) * HALF, D:ROW])
            last.then_inc(s("xq_columns"), 1)
            quad(0, 0, 0, first=True)
            link(nc.vector.tensor_tensor(eidf, over_t(cnt[:, a_, :], NS),
                                         bcast(iotk[:, :], 2, E), ALU.is_le))
            link(nc.vector.tensor_reduce(out=iotk[:, :], in_=eidf, axis=AX, op=ALU.add))
            nc.vector.tensor_scalar(eid_i[:, 2:NS + 2], iotk[:, :], float(E - 1), None, ALU.min).then_inc(s("eid_ready"), 1)
            quad(1, 0, 1)
            with dve.Fori(1, NCH - 1, 1) as c:
                quad(2 * c, c, 0)
                quad(2 * c + 1, c, 1)
            quad(NQ - 2, NCH - 1, 0, ahead=False)
            quad(NQ - 1, NCH - 1, 1, more=False, ahead=False)

            dve.wait_ge(s("eid_ready"), 1)
            dve.wait_ge(s("b2_in"), 16)
            dve.wait_ge(s("b1b_ready"), E)
            dve.wait_ge(s("qk_ps"), NT)
            def se_x_low(k, a):
                dve.wait_ge(s("sex_sb"), k + 1)
                reach(dve, s("h_ps"), k - 1)
                nc.vector.tensor_tensor(xse[:, a % 2, 1, :], banks[6 + a % 2][:, 0:P], xse[:, a % 2, 0, :].bitcast(F32),
                                        ALU.subtract).then_inc(s("sex_lo"), 1)

            def se_bias(k, a, e):
                dve.wait_ge(s("h_ps"), k + 1)
                reach(dve, s("ht_ps"), k - 1)
                nc.vector.scalar_tensor_tensor(out=hb[:, a % 2, :], in0=banks[a % 2][:, :], scalar=xs[:, a, D:D + 1],
                                               in1=b1b[:, e, :], op0=ALU.mult, op1=ALU.add).then_inc(s("hb_ready"), 1)

            def se_result(k, a, rnd, e):
                reach(dve, s(f"out_done{a}"), 16 * rnd)
                nc.vector.tensor_scalar(idxe[:, a:a + 1], xs[:, a, D + 2:D + 3], -1.0, float(NTOK), ALU.mult, ALU.add)
                dve.wait_ge(s("ye_ps"), k + 1)
                nc.vector.tensor_tensor(yb[:, a % 2, :], banks[4 + a % 2][:, 0:D], b2b[:, e, :], ALU.add)\
                    .then_inc(s("yb_done"), 1)
                dve.wait_ge(s("yb_done"), k + 1)
                nc.vector.tensor_scalar(ye[:, a, :], yb[:, a % 2, :], xs[:, a, D + 1:D + 2], None, ALU.mult)\
                    .then_inc(s("ye_ready"), 1)

            def expert_round(i, e, first=False, last=False):
                for a in range(RING):
                    k = RING * i + a
                    if not last or a < RING - 1:
                        se_bias(k + 1, (a + 1) % RING, e[a + 3])
                    if a > 1:
                        se_result(k - 2, a - 2, i, e[a])
                    elif not first:
                        se_result(k - 2, RING - 2 + a, i - 1, e[a])
                    if not last or a + 3 < RING:
                        se_x_low(k + 3, a + 3)

            result(NQ - 1, NCH - 1, 1)
            regs = expert_registers(dve)
            e = load_experts(dve, regs, 0)
            se_x_low(0, 0)
            se_x_low(1, 1)
            se_bias(0, 0, e[2])
            se_x_low(2, 2)
            expert_round(0, e, first=True)
            with dve.Fori(1, ROUNDS - 1, 1) as i:
                expert_round(i, load_experts(dve, regs, i))
            e = load_experts(dve, regs, ROUNDS - 1)
            expert_round(ROUNDS - 1, e, last=True)
            se_result(NS - 2, RING - 2, ROUNDS - 1, e[RING])
            se_result(NS - 1, RING - 1, ROUNDS - 1, e[RING + 1])

        @block.tensor
        def _(pe):
            mm = nc.tensor.matmul
            pe.wait_ge(s("ident_ready"), 1)
            pe.wait_ge(s("cen_in"), 16)

            pe.wait_ge(s("ones_ready"), 1)
            pe.wait_ge(s("wq_sq"), 1)
            mm(banks[6][:, 0:D], ones[:, :], sq[:, 0:D], start=True, stop=True).then_inc(s("norm_ps"), 1)

            def ln_transpose(c, a):
                pe.wait_ge(s("lnx_ready"), c + 1)
                for hf in range(2):
                    reach(pe, s("xta_sb"), 2 * (c - 1) + hf + 1)
                    for b in range(HALF):
                        last = nc.tensor.transpose(banks[hf][:, b * P:(b + 1) * P], lnx[:, a, hf * HALF + b, :], ident[:, :])
                    last.then_inc(s("xta_ps"), 1)

            def affinities(c, a, i):
                if a == 0:
                    reach(pe, s("aff_sb"), i)
                for hf in range(2):
                    g = 2 * a + hf
                    pe.wait_ge(s("xta_sb"), 2 * c + hf + 1)
                    mm(banks[7][32 * g:32 * (g + 1), :], cen_t[:, :], xta[:, hf, :, :].rearrange("p b t -> p (b t)"),
                       start=True, stop=True).then_inc(s("aff_ps"), 1)

            def affinity_transpose(i):
                pe.wait_ge(s("aff_sb"), i + 1)
                reach(pe, s("aff_in"), i)
                for b in range(HALF):
                    last = nc.tensor.transpose(banks[5][:, b * P:(b + 1) * P], afft[:, b * P:(b + 1) * P], ident[:, :])
                last.then_inc(s("aff_t"), 1)

            def prep_transpose(e, a, i):
                pe.wait_ge(s(f"wraw_in{a}"), 48 * (i + 1))
                reach(pe, s("w1t_ready"), e)
                for c in range(FC):
                    last = nc.tensor.transpose(banks[2][:, c * P:(c + 1) * P], w1raw[:, a, c, :], ident[:, :])
                last.then_inc(s("w1t_ps"), 1)
                reach(pe, s("w2t_ready"), e)
                for c in range(FC):
                    last = nc.tensor.transpose(banks[3][:, c * P:(c + 1) * P], w2raw[:, a, c * P:(c + 1) * P], ident[:, :])
                last.then_inc(s("w2t_ps"), 1)

            def prep_bias(e, a):
                pe.wait_ge(s("w1tr_ready"), e + 1)
                reach(pe, s("b1b_ready"), e)
                mm(banks[4][:, :], lbb, w1tr, start=True, stop=False)
                mm(banks[4][:, :], ones[0:1, :], b1row[a], start=False, stop=True).then_inc(s("b1_ps"), 1)

            def chunk(c, a, i, first=False):
                ln_transpose(c, a)
                if not first:
                    prep_bias(c - 1, 1 - a)
                affinities(c, a, i)
                if a == 0 and not first:
                    affinity_transpose(i - 1)
                prep_transpose(c, a, i)

            chunk(0, 0, 0, first=True)
            chunk(1, 1, 0)
            with pe.Fori(1, NCH // 2, 1) as i:
                for a in range(2):
                    chunk(2 * i + a, a, i)

            def x_trans(n, par):
                pe.wait_ge(s("xq_ready"), n + 1)
                reach(pe, s("qt_sb"), n)
                for i in range(HALF):
                    last = nc.tensor.transpose(EB[:, i * P:(i + 1) * P], xq[:, par, i, 0:D], ident[:, :])
                last.then_inc(s("xt_ps"), 1)

            def project(bank, col, done):
                for i in range(HALF):
                    last = mm(bank[:, i * P:(i + 1) * P], xt[:, i, :], wqkv[:, col:col + D], start=True, stop=True)
                last.then_inc(s(done), 1)

            def q_project(n):
                reach(pe, s("ds_sb"), n - 1)
                project(CB, 0, "q_ps")

            def k_project(n):
                pe.wait_ge(s("xt_sb"), n + 1)
                project(EB, D, "k_ps")

            def v_project(n):
                pe.wait_ge(s("q_sb"), n + 1)
                project(CB, 2 * D, "v_ps")

            def q_trans(n):
                pe.wait_ge(s("k_sb"), n + 1)
                for i in range(HALF):
                    last = nc.tensor.transpose(EB[:, i * P:(i + 1) * P], q32[:, i * D:(i + 1) * D], ident[:, :])
                last.then_inc(s("qt_ps"), 1)

            def qk_trans(m, n, i, par):
                if i == 0:
                    pe.wait_ge(s("q_parts"), n + 1)
                    pe.wait_ge(s("k_parts"), n + 1)
                reach(pe, s("qq_sb"), m)
                reach(pe, s("kk_sb"), m)
                for j in range(J):
                    h0 = i * H + j * G
                    qv = qs[:, par, h0:h0 + G, :, :].rearrange("p g r d -> p (g r d)")
                    nc.tensor.transpose(qb16[:, j, :], qv, identh[:, :])
                    kv = ks[:, par, h0:h0 + G, :, :].rearrange("p g r d -> p (g r d)")
                    last = nc.tensor.transpose(kb16[:, j, :], kv, identh[:, :])
                last.then_inc(s("qk_ps"), 1)

            def scores(m, i, g):
                if g == 0:
                    pe.wait_ge(s("qq_sb"), m + 1)
                    pe.wait_ge(s("kk_sb"), m + 1)
                reach(pe, s("pr_odd" if g % 2 else "sc_even"), 2 * m + g // 2)
                for j in range(J):
                    last = mm(SC[g % 2][:, j * P:(j + 1) * P], kkt[32 * g:32 * (g + 1), i % 2, j, :],
                              qqt[32 * g:32 * (g + 1), i % 2, j, :], start=True, stop=True)
                last.then_inc(s("sc_ps"), 1)

            def inter(m, n, i, par):
                if i == 0:
                    pe.wait_ge(s("qt_sb"), n + 1)
                    reach(pe, s("state_ready"), n - 1)
                reach(pe, s("y_sb"), m)
                mm(YB[:, 0:P], state[:, par * HALF + i, :], qt[:, par, i, :], start=True, stop=False)

            def weighted(m, i, par, g):
                if g == 0:
                    pe.wait_ge(s("vz_ready"), m + 1)
                pe.wait_ge(s("pr_odd" if g % 2 else "pr_even"), 2 * m + g // 2 + 1)
                for j in range(J):
                    last = mm(YB[32 * g:32 * (g + 1), 0:P], vz[:, i % 2, j, 32 * g:32 * (g + 1)],
                              pr[:, g, j * P:(j + 1) * P], start=False, stop=(j == J - 1))
                last.then_inc(s("av_ps"), 1)

            def output(m, n, i):
                if i == 0:
                    reach(pe, s("res_ready"), n)
                pe.wait_ge(s("y_sb"), m + 1)
                mm(DB[:, i * D:(i + 1) * D], y[:, i % 2, :], wo[:, :], start=True, stop=True).then_inc(s("out_ps"), 1)

            def state_step(n, par):
                pe.wait_ge(s("v_sb"), n + 2)
                for i in range(HALF):
                    last = mm(CB[:, i * P:(i + 1) * P], k32[:, par, i * D:(i + 1) * D], v32[:, par, i * D:(i + 1) * D],
                              start=True, stop=True)
                last.then_inc(s("ds_ps"), 1)

            def quad(n, c, half, first=False, more=True, ahead=True):
                other = 1 - half
                for i in range(HALF):
                    m = 4 * n + i
                    before = not (first and i == 0)
                    i_b, par_b = (i - 1) % HALF, half if i else other
                    scores(m, i, 0)
                    if before:
                        weighted(m - 1, i_b, par_b, 2)
                    if i < 3:
                        qk_trans(m + 1, n, i + 1, half)
                    if ahead and i == 3:
                        state_step(n, half)
                    scores(m, i, 1)
                    if before:
                        weighted(m - 1, i_b, par_b, 3)
                    if more and i == 0:
                        x_trans(n + 1, other)
                    if more and i == 1:
                        q_project(n + 1)
                    if more and i == 2:
                        v_project(n + 1)
                    if more and i == 3:
                        qk_trans(m + 1, n + 1, 0, other)
                    scores(m, i, 2)
                    inter(m, n, i, half)
                    weighted(m, i, half, 0)
                    if more and i == 0:
                        k_project(n + 1)
                    if more and i == 2:
                        q_trans(n + 1)
                    scores(m, i, 3)
                    weighted(m, i, half, 1)
                    if before:
                        output(m - 1, n if i else n - 1, i_b)
            pe.wait_ge(s("wqkv_ready"), 1)
            pe.wait_ge(s("wo_ready"), 1)
            affinity_transpose(NCH // 2 - 1)
            prep_bias(E - 1, 1)
            x_trans(0, 0)
            k_project(0)
            pe.wait_ge(s("aff_in"), NCH // 2)
            q_project(0)
            pe.wait_ge(s("xta_sb"), 2 * NCH)
            pe.wait_ge(s("scan_ready"), 1)
            total = scan[:, 1, :, :]
            mm(banks[0][:, :], notbefore[:, :], ohb[:, :, :].rearrange("p t e -> p (t e)"), start=True, stop=False)
            mm(banks[0][:, :], onesb[:, :], total.rearrange("p t e -> p (t e)"), start=False, stop=True)\
                .then_inc(s("rank_ps"), 1)
            mm(banks[1][:, 0:E], onesb[:, :], total[:, NT - 1, :], start=True, stop=True).then_inc(s("rank_ps"), 1)
            v_project(0)
            q_trans(0)
            pe.wait_ge(s("b1b_ready"), E)
            pe.wait_ge(s("w2t_ready"), E)
            qk_trans(0, 0, 0, 0)
            pe.wait_ge(s("state_zero"), 1)
            pe.wait_ge(s("route_done"), 1)
            quad(0, 0, 0, first=True)
            quad(1, 0, 1)
            with pe.Fori(1, NCH - 1, 1) as c:
                quad(2 * c, c, 0)
                quad(2 * c + 1, c, 1)
            quad(NQ - 2, NCH - 1, 0, ahead=False)
            quad(NQ - 1, NCH - 1, 1, more=False, ahead=False)
            weighted(NT - 1, HALF - 1, 1, 2)
            weighted(NT - 1, HALF - 1, 1, 3)
            output(NT - 1, NQ - 1, HALF - 1)

            pe.wait_ge(s("y_sb"), NT)
            pe.wait_ge(s("w1_lo"), E)
            pe.wait_ge(s("w2t_ready"), E)
            pe.wait_ge(s("eid_ready"), 1)

            def se_trans(k, a, rnd):
                pe.wait_ge(s(f"se_in{a}"), 16 * (rnd + 1))
                reach(pe, s("sex_lo"), k - 1)
                nc.tensor.transpose(banks[6 + a % 2][:, 0:P], xs[:, a, 0:D], ident[:, :]).then_inc(s("sex_ps"), 1)

            def se_up(k, a, e):
                pe.wait_ge(s("sex_lo"), k + 1)
                reach(pe, s("hb_ready"), k - 1)
                h = banks[a % 2][:, :]
                high, low = xse[:, a % 2, 0, :], xse[:, a % 2, 1, :]
                mm(h, high, w1h[:, e, :], start=True, stop=False)
                mm(h, high, w1l[:, e, :], start=False, stop=False)
                mm(h, low, w1h[:, e, :], start=False, stop=True).then_inc(s("h_ps"), 1)

            def se_hidden(k, a):
                pe.wait_ge(s("hb_ready"), k + 1)
                reach(pe, s("ht_sb"), k - 1)
                for c in range(FC):
                    last = nc.tensor.transpose(banks[2 + a % 2][:, c * P:(c + 1) * P], hb[:, a % 2, c * P:(c + 1) * P],
                                               ident[:, :])
                last.then_inc(s("ht_ps"), 1)

            def se_down(k, a, e):
                pe.wait_ge(s("ht_sb"), k + 1)
                reach(pe, s("yb_done"), k - 1)
                for c in range(FC):
                    last = mm(banks[4 + a % 2][:, 0:D], ht[:, a % 2, c * P:(c + 1) * P], w2t[:, e, c, :],
                              start=(c == 0), stop=(c == FC - 1))
                last.then_inc(s("ye_ps"), 1)

            def expert_round(i, e, first=False, last=False):
                for a in range(RING):
                    k = RING * i + a
                    if not last or a < RING - 1:
                        se_up(k + 1, (a + 1) % RING, e[a + 3])
                    if not last or a < RING - 3:
                        se_trans(k + 3, (a + 3) % RING, i + (a + 3) // RING)
                    if not (first and a < 2):
                        se_down(k - 2, (a - 2) % RING, e[a])
                    se_hidden(k, a)

            se_trans(0, 0, 0)
            pe.wait_ge(s("res_ready"), NQ)
            se_trans(1, 1, 0)
            regs = expert_registers(pe)
            e = load_experts(pe, regs, 0)
            se_up(0, 0, e[2])
            se_trans(2, 2, 0)
            expert_round(0, e, first=True)
            with pe.Fori(1, ROUNDS - 1, 1) as i:
                expert_round(i, load_experts(pe, regs, i))
            e = load_experts(pe, regs, ROUNDS - 1)
            expert_round(ROUNDS - 1, e, last=True)
            se_down(NS - 2, RING - 2, e[RING])
            se_down(NS - 1, RING - 1, e[RING + 1])


_INS = ["L0_attn_x", "L0_attn_W_qkv", "L0_attn_W_o", "L0_ffn_centroids", "L0_ffn_ln_g", "L0_ffn_ln_b", "L0_ffn_w1",
        "L0_ffn_b1", "L0_ffn_w2", "L0_ffn_b2"]


def kernel(**inputs):
    import numpy as _np
    import concourse.bacc as _bacc
    from concourse import mybir as _mybir
    from concourse.bass_utils import run_bass_kernel_spmd as _run

    nc = _bacc.Bacc("TRN2", target_bir_lowering=False, num_devices=1)
    arrays, args = {}, []
    for name in _INS:
        a = _np.ascontiguousarray(inputs[name])
        arrays[f"in_{name}_dram"] = a
        args.append(nc.dram_tensor(f"in_{name}_dram", a.shape, _mybir.dt.from_np(a.dtype), kind="ExternalInput").ap())
    args.append(nc.dram_tensor("out_dram", inputs["L0_attn_x"].shape, _mybir.dt.from_np(_np.dtype("float32")),
                               kind="ExternalOutput").ap())
    moe_attention_kernel(nc, *args)
    r = _run(nc, [arrays], core_ids=[0])
    return r.results[0]["out_dram"]
```
